# Optimizing a Trainium2 kernel written in Bass

```python
import numpy as np
import jax
import jax.numpy as jnp

def _softmax(x, axis=-1):
    return jax.nn.softmax(x, axis=axis)

def _gelu(x):
    return jax.nn.gelu(x, approximate=True)

def _silu(x):
    return jax.nn.silu(x)

def _sigmoid(x):
    return jax.nn.sigmoid(x)

def _layernorm(x, axis=-1, eps=1e-05):
    m = jnp.mean(x, axis=axis, keepdims=True)
    v = jnp.var(x, axis=axis, keepdims=True)
    return (x - m) / jnp.sqrt(v + eps)

def _scatter_add(tgt, idx, src, axis=0):
    return tgt.at[idx].add(src)

def _segment_sum(src, seg, n):
    return jax.ops.segment_sum(src, seg, n)
kernel_name = 'mk_flamingo_gated_d2_seqx_r8_fbb3c4'

def setup_inputs(seed: int=0):
    np.random.seed(seed)
    _w = jnp.asarray

    def _rec_inputs():
        import jax
        import jax.numpy as jnp
        _rk = jax.random.key(seed)
        x = 7.22e-05 + 1 * jax.random.normal(jax.random.fold_in(_rk, 1), (16, 128, 256), jnp.float32)
        _lenS = 128 - jax.random.randint(jax.random.fold_in(_rk, 7), (16,), 0, max(1, 128 // 4) + 1, jnp.int32)
        _lenS2 = 128 - jax.random.randint(jax.random.fold_in(_rk, 8), (16,), 0, max(1, 128 // 4) + 1, jnp.int32)
        _ctx_2048P = jax.random.normal(jax.random.fold_in(_rk, 11), (16, 16, 256), jnp.float32)
        _ctx_2048c = jax.random.dirichlet(jax.random.fold_in(_rk, 511), 0.3 * jnp.ones((16,), jnp.float32), (16, 128))
        _ctx_2048t = jnp.einsum('bsk,bkd->bsd', _ctx_2048c, _ctx_2048P)
        _ctx_2048t = _ctx_2048t * jax.lax.rsqrt(jnp.mean(jnp.square(_ctx_2048t)) + 1e-12) * 0.953939
        ctx_2048 = 4.13588e-05 + 0.999923 * (_ctx_2048t + 0.3 * jax.random.normal(jax.random.fold_in(_rk, 611), (16, 128, 256), jnp.float32))
        _g = jax.random.normal(jax.random.fold_in(_rk, 9001), (2, 2), jnp.float32)
        _g = jnp.sign(_g) * jnp.maximum(jnp.abs(_g), 1.0) + (_g == 0) * 1.0
        g_xattn = _g[0]
        g_ffn = _g[1]
        return (x, ctx_2048, g_xattn, g_ffn)
    x, ctx_2048, g_xattn, g_ffn = _rec_inputs()

    def _L0_xattn_setup():
        import jax, jax.numpy as jnp
        import numpy as np
        BS, S, DK = (8, 64, 256)
        key = jax.random.key(seed)
        kq, kk, kv = jax.random.split(key, 3)
        q = jax.random.normal(kq, (BS, S, DK), dtype=jnp.float32)
        k = jax.random.normal(kk, (BS, S, DK), dtype=jnp.float32)
        v = jax.random.normal(kv, (BS, S, DK), dtype=jnp.float32)
        return {'q': q, 'k': k, 'v': v}
    _L0_xattn_all = _L0_xattn_setup()
    _L0_xattn_in = {k: v for k, v in _L0_xattn_all.items() if k in ()}
    del _L0_xattn_all

    def _L0_ffn_setup():
        import jax, jax.numpy as jnp
        import numpy as np
        TARGET_SPARSITY = 0.9
        LN_EPS = 1e-05

        def ternary_quant(W):
            scale = jnp.mean(jnp.abs(W))
            q = jnp.clip(jnp.round(W / (scale + 1e-08)), -1.0, 1.0) * scale
            return W + jax.lax.stop_gradient(q - W)

        def layernorm(x, gamma, beta):
            mu = jnp.mean(x, axis=-1, keepdims=True)
            var = jnp.var(x, axis=-1, keepdims=True)
            return (x - mu) * jax.lax.rsqrt(var + LN_EPS) * gamma + beta
        key = jax.random.key(seed)
        ks = jax.random.split(key, 3)
        B, S, D, N = (4, 256, 256, 1024)
        x = jax.random.normal(ks[0], (B, S, D), dtype=jnp.float32)
        W_syn = jax.random.normal(ks[1], (N, D), dtype=jnp.float32) * (1.0 / np.sqrt(D))
        b_syn = jnp.zeros((N,), dtype=jnp.float32)
        W_out = jax.random.normal(ks[2], (D, N), dtype=jnp.float32) * (1.0 / np.sqrt(N))
        b_out = jnp.zeros((D,), dtype=jnp.float32)
        gamma = jnp.ones((D,), dtype=jnp.float32)
        beta = jnp.zeros((D,), dtype=jnp.float32)
        return {'x': x, 'W_syn': W_syn, 'b_syn': b_syn, 'W_out': W_out, 'b_out': b_out, 'gamma': gamma, 'beta': beta}
    _L0_ffn_all = _L0_ffn_setup()
    _L0_ffn_in = {k: v for k, v in _L0_ffn_all.items() if k in ('W_syn', 'b_syn', 'W_out', 'b_out', 'gamma', 'beta')}
    del _L0_ffn_all

    def _L1_xattn_setup():
        import jax, jax.numpy as jnp
        import numpy as np
        key = jax.random.key(seed)
        k1, k2, k3, k4, k5 = jax.random.split(key, 5)
        B, D_MODEL, L = (2, 128, 256)
        HEAD_DIM = 8
        H = D_MODEL // HEAD_DIM
        return {'k': jax.random.normal(k1, (B, D_MODEL, L), dtype=jnp.float32), 'v': jax.random.normal(k2, (B, D_MODEL, L), dtype=jnp.float32), 'q': jax.random.normal(k3, (B, D_MODEL, L), dtype=jnp.float32), 'ssm_kernel': jax.random.normal(k4, (H, L), dtype=jnp.float32), 'D': jax.random.normal(k5, (H,), dtype=jnp.float32), 'head_dim': HEAD_DIM}
    _L1_xattn_all = _L1_xattn_setup()
    _L1_xattn_in = {k: v for k, v in _L1_xattn_all.items() if k in ('ssm_kernel', 'D')}
    del _L1_xattn_all

    def _L1_ffn_setup():
        import jax, jax.numpy as jnp
        import numpy as np
        HIDDEN = 256
        FFN = 176
        N_EXPERTS = 64
        TOP_K = 6
        N_SHARED = 2
        SHARED_FFN = FFN * N_SHARED
        ROUTED_SCALING = 1.0
        EPS = 1e-20

        def _moe_forward(x, gate_w, w_gate_up, w_down, ws_gate_up, ws_down):
            T = x.shape[0]
            logits = jnp.einsum('th,eh->te', x.astype(jnp.float32), gate_w.astype(jnp.float32))
            scores = jax.nn.softmax(logits, axis=-1)
            topk_w, topk_ids = jax.lax.top_k(scores, TOP_K)
            topk_w = topk_w / (jnp.sum(topk_w, axis=-1, keepdims=True) + EPS)
            topk_w = topk_w * ROUTED_SCALING
            comb = jnp.zeros((T, N_EXPERTS), dtype=x.dtype)
            comb = comb.at[jnp.arange(T)[:, None], topk_ids].add(topk_w.astype(x.dtype))
            gu = jnp.einsum('th,efh->tef', x, w_gate_up)
            g, u = (gu[..., :FFN], gu[..., FFN:])
            act = jax.nn.silu(g) * u
            act = act * comb[:, :, None]
            routed = jnp.einsum('tef,ehf->th', act, w_down)
            sgu = jnp.einsum('th,fh->tf', x, ws_gate_up)
            sg, su = (sgu[..., :SHARED_FFN], sgu[..., SHARED_FFN:])
            shared = jnp.einsum('tf,hf->th', jax.nn.silu(sg) * su, ws_down)
            return routed + shared
        key = jax.random.key(seed)
        k0, k1, k2, k3, k4, k5 = jax.random.split(key, 6)
        hidden_states = jax.random.normal(k0, (1, 32, HIDDEN), dtype=jnp.float32)
        gate_w = jax.random.normal(k1, (N_EXPERTS, HIDDEN), dtype=jnp.float32) * 0.05
        w_gate_up = jax.random.normal(k2, (N_EXPERTS, 2 * FFN, HIDDEN), dtype=jnp.float32) * 0.02
        w_down = jax.random.normal(k3, (N_EXPERTS, HIDDEN, FFN), dtype=jnp.float32) * 0.02
        ws_gate_up = jax.random.normal(k4, (2 * SHARED_FFN, HIDDEN), dtype=jnp.float32) * 0.02
        ws_down = jax.random.normal(k5, (HIDDEN, SHARED_FFN), dtype=jnp.float32) * 0.02
        return {'hidden_states': hidden_states, 'gate_w': gate_w, 'w_gate_up': w_gate_up, 'w_down': w_down, 'ws_gate_up': ws_gate_up, 'ws_down': ws_down}
    _L1_ffn_all = _L1_ffn_setup()
    _L1_ffn_in = {k: v for k, v in _L1_ffn_all.items() if k in ('gate_w', 'w_gate_up', 'w_down', 'ws_gate_up', 'ws_down')}
    del _L1_ffn_all
    return {'x': x, 'ctx_2048': ctx_2048, 'g_xattn': g_xattn, 'g_ffn': g_ffn, 'L0_ffn_W_syn': _L0_ffn_in['W_syn'], 'L0_ffn_b_syn': _L0_ffn_in['b_syn'], 'L0_ffn_W_out': _L0_ffn_in['W_out'], 'L0_ffn_b_out': _L0_ffn_in['b_out'], 'L0_ffn_gamma': _L0_ffn_in['gamma'], 'L0_ffn_beta': _L0_ffn_in['beta'], 'L1_xattn_ssm_kernel': _L1_xattn_in['ssm_kernel'], 'L1_xattn_D': _L1_xattn_in['D'], 'L1_ffn_gate_w': _L1_ffn_in['gate_w'], 'L1_ffn_w_gate_up': _L1_ffn_in['w_gate_up'], 'L1_ffn_w_down': _L1_ffn_in['w_down'], 'L1_ffn_ws_gate_up': _L1_ffn_in['ws_gate_up'], 'L1_ffn_ws_down': _L1_ffn_in['ws_down']}

def reference(x, ctx_2048, g_xattn, g_ffn, L0_ffn_W_syn, L0_ffn_b_syn, L0_ffn_W_out, L0_ffn_b_out, L0_ffn_gamma, L0_ffn_beta, L1_xattn_ssm_kernel, L1_xattn_D, L1_ffn_gate_w, L1_ffn_w_gate_up, L1_ffn_w_down, L1_ffn_ws_gate_up, L1_ffn_ws_down):
    import jax
    import jax.numpy as jnp

    def _L0_xattn_ref(q, k, v):
        import jax, jax.numpy as jnp
        import numpy as np
        BS, S, DK = (8, 64, 256)
        dk = q.shape[-1]
        scale = 1.0 / jnp.sqrt(jnp.asarray(dk, dtype=q.dtype))
        scaled = jnp.einsum('bsd,bse->bde', q, k) * scale
        attn = jax.nn.softmax(scaled, axis=1)
        out = jnp.einsum('bde,bse->bsd', attn, v)
        return out

    def _L0_ffn_ref(x, W_syn, b_syn, W_out, b_out, gamma, beta):
        import jax, jax.numpy as jnp
        import numpy as np
        TARGET_SPARSITY = 0.9
        LN_EPS = 1e-05

        def ternary_quant(W):
            scale = jnp.mean(jnp.abs(W))
            q = jnp.clip(jnp.round(W / (scale + 1e-08)), -1.0, 1.0) * scale
            return W + jax.lax.stop_gradient(q - W)

        def layernorm(x, gamma, beta):
            mu = jnp.mean(x, axis=-1, keepdims=True)
            var = jnp.var(x, axis=-1, keepdims=True)
            return (x - mu) * jax.lax.rsqrt(var + LN_EPS) * gamma + beta
        B, S, D = x.shape
        N = W_syn.shape[0]
        x_flat = x.reshape(-1, D)
        z = x_flat @ ternary_quant(W_syn).T + b_syn
        k = max(1, int(N * (1.0 - TARGET_SPARSITY)))
        topv, _ = jax.lax.top_k(z, k)
        thresh = topv[:, -1:]
        hidden = jnp.where(z >= thresh, jax.nn.relu(z), 0.0)
        out = hidden @ ternary_quant(W_out).T + b_out
        out = out.reshape(B, S, D)
        return layernorm(x + out, gamma, beta)

    def _L1_xattn_ref(k, v, q, ssm_kernel, D, head_dim):
        import jax, jax.numpy as jnp
        import numpy as np
        B, HD, L = k.shape
        H = HD // head_dim
        fft_size = 2 * L
        k_ = k.reshape(B, H, head_dim, L)
        v_ = v.reshape(B, H, head_dim, L)
        q_ = q.reshape(B, H, head_dim, L)
        kv = jnp.einsum('bhil,bhjl->bijhl', k_, v_)
        kv_f = jnp.fft.rfft(kv, n=fft_size)
        kernel_f = jnp.fft.rfft(ssm_kernel, n=fft_size)
        y = jnp.fft.irfft(kv_f * kernel_f, n=fft_size)[..., :L]
        out = y + kv * D[None, None, None, :, None]
        out = jnp.einsum('bijhl,bhil->bjhl', out, q_)
        out = jnp.transpose(out, (0, 2, 1, 3)).reshape(B, H * head_dim, L)
        return out.astype(k.dtype)

    def _L1_ffn_ref(hidden_states, gate_w, w_gate_up, w_down, ws_gate_up, ws_down):
        import jax, jax.numpy as jnp
        import numpy as np
        HIDDEN = 256
        FFN = 176
        N_EXPERTS = 64
        TOP_K = 6
        N_SHARED = 2
        SHARED_FFN = FFN * N_SHARED
        ROUTED_SCALING = 1.0
        EPS = 1e-20

        def _moe_forward(x, gate_w, w_gate_up, w_down, ws_gate_up, ws_down):
            T = x.shape[0]
            logits = jnp.einsum('th,eh->te', x.astype(jnp.float32), gate_w.astype(jnp.float32))
            scores = jax.nn.softmax(logits, axis=-1)
            topk_w, topk_ids = jax.lax.top_k(scores, TOP_K)
            topk_w = topk_w / (jnp.sum(topk_w, axis=-1, keepdims=True) + EPS)
            topk_w = topk_w * ROUTED_SCALING
            comb = jnp.zeros((T, N_EXPERTS), dtype=x.dtype)
            comb = comb.at[jnp.arange(T)[:, None], topk_ids].add(topk_w.astype(x.dtype))
            gu = jnp.einsum('th,efh->tef', x, w_gate_up)
            g, u = (gu[..., :FFN], gu[..., FFN:])
            act = jax.nn.silu(g) * u
            act = act * comb[:, :, None]
            routed = jnp.einsum('tef,ehf->th', act, w_down)
            sgu = jnp.einsum('th,fh->tf', x, ws_gate_up)
            sg, su = (sgu[..., :SHARED_FFN], sgu[..., SHARED_FFN:])
            shared = jnp.einsum('tf,hf->th', jax.nn.silu(sg) * su, ws_down)
            return routed + shared
        B, S, H = hidden_states.shape
        x = hidden_states.reshape(-1, H)
        out = _moe_forward(x, gate_w, w_gate_up, w_down, ws_gate_up, ws_down)
        return out.reshape(B, S, H)
    x = x + jnp.tanh(g_xattn[0]) * _L0_xattn_ref(_layernorm(x, axis=-1), ctx_2048, ctx_2048)
    x = x + jnp.tanh(g_ffn[0]) * _L0_ffn_ref(_layernorm(x, axis=-1), L0_ffn_W_syn, L0_ffn_b_syn, L0_ffn_W_out, L0_ffn_b_out, L0_ffn_gamma, L0_ffn_beta)
    x = x + jnp.tanh(g_xattn[1]) * _L1_xattn_ref(ctx_2048, ctx_2048, _layernorm(x, axis=-1), L1_xattn_ssm_kernel, L1_xattn_D, 8)
    x = x + jnp.tanh(g_ffn[1]) * _L1_ffn_ref(_layernorm(x, axis=-1), L1_ffn_gate_w, L1_ffn_w_gate_up, L1_ffn_w_down, L1_ffn_ws_gate_up, L1_ffn_ws_down)
    return x

_drawn_inputs = setup_inputs


def setup_inputs(seed=0):
    import zlib

    import numpy as np

    out = dict(_drawn_inputs(seed))
    spreads = {'g_ffn': (-1.0, 0.6),
     'L0_ffn_b_syn': (0.0, 0.1),
     'L0_ffn_b_out': (0.0, 0.1),
     'L0_ffn_gamma': (1.0, 0.2),
     'L0_ffn_beta': (0.0, 0.1)}
    factors = {'L1_ffn_gate_w': 8.0,
     'L1_ffn_w_gate_up': 8.0,
     'L1_ffn_w_down': 8.0,
     'L1_ffn_ws_gate_up': 8.0,
     'L1_ffn_ws_down': 8.0}
    for name, (base, spread) in spreads.items():
        noise = np.random.default_rng([zlib.crc32(name.encode()), seed]).standard_normal(out[name].shape)
        drawn = base * np.exp(spread * noise) if base else spread * noise
        out[name] = jnp.asarray(drawn.astype(out[name].dtype))
    for name, factor in factors.items():
        out[name] = (out[name] * factor).astype(out[name].dtype)
    return out
```

```python
import concourse.bass as bass
from concourse import mybir
from contextlib import ExitStack


def build(nc, x, ctxn, ctxT, ctxH, toep, gates_in, wsynT, woutT, bsyn, bout, gamma, beta, ssm_D,
          gateT, wexp, wd1, wsgu, wsd, out):
    f32, bf16, i32, u32 = mybir.dt.float32, mybir.dt.bfloat16, mybir.dt.int32, mybir.dt.uint32
    ALU = mybir.AluOpType
    ACT = mybir.ActivationFunctionType
    AX = mybir.AxisListType

    P = 128
    NT = 16
    D = 256
    N = 1024
    NH, HD = 16, 8
    NPR = HD * (HD + 1) // 2
    TOPK = 102
    ROUNDS = 5
    AIM, NEAR = TOPK - 4, TOPK - 8
    FAR = 60.0
    SIG = 13.3
    DENS = N * 0.1755
    NTD = 8

    T = NT * P
    E = 64
    K = 6
    F = 176
    F1 = F - P
    GU = 368
    CAP = 256
    ROW = 272
    CT, CE, CW = D, D + 1, D + 1 + K
    FS = [(0, P), (P, P), (2 * P, 96)]
    FSH = 352
    MAXB = 96
    NPAIR = NT // 2

    xs_rows = nc.dram_tensor("xs_rows", (E * T + P, ROW), f32, kind="Internal").ap()
    rows_v = xs_rows[0:E * T, :].rearrange("(e c) d -> e c d", c=T)
    acc = [nc.dram_tensor(f"acc{i}", (T + P, D), f32, kind="Internal").ap() for i in range(4)]

    with ExitStack() as ctx:
        def sb(name, shape, dt=f32):
            return ctx.enter_context(nc.sbuf_tensor(name, shape, dt))

        def sem(name):
            return ctx.enter_context(nc.semaphore(name))

        X = sb("X", [P, NT, D])
        Z = sb("Z", [P, NT * N])
        z = Z[:, :].rearrange("p (t n) -> p t n", n=N)
        wraw = Z[:, 0:4 * N].rearrange("p (a n) -> p a n", a=4)
        prods = Z[:, 8448:8448 + 4096].rearrange("p (a n) -> p a n", a=2)
        kv = Z[:, 12544:12544 + 4 * NT * NPR].rearrange("p (a m b r) -> p a m b r", a=2, m=2, b=NT)
        H2 = sb("H2", [P, NT, D])
        OT = H2[:, :, :].rearrange("p b (c d) -> p (b c) d", c=2).rearrange("p (l b) d -> p l b d", l=2)
        qT = sb("qT", [P, 2, NT, P])
        wt = sb("wt", [P, 4, N])
        wsyn = wt[:, 0:2, :]
        wout = wt[:, 2:4, :].rearrange("p a n -> p (a n)").rearrange("p (c d) -> p c d", c=8)
        hidden = sb("hidden", [P, 2, N])
        hidT = sb("hidT", [P, 2, N])
        attn = hidT[:, 0, :].rearrange("p (a e d) -> p a e d", a=2, e=2)
        qn = hidT[:, 1, 0:512].rearrange("p (a d) -> p a d", a=2)
        vTs = hidT[:, 1, 512:1024].rearrange("p (a e s) -> p a e s", a=2, e=2)
        ctx_s = sb("ctx_s", [P, 2, D])
        ctxT_s = sb("ctxT_s", [P, 2, 2, P])
        ctxH_s = sb("ctxH_s", [P, 2, 2, NT, HD])
        toep_s = sb("toep_s", [P, 2, 2, P])
        tdiag = sb("tdiag", [P, 2, P])
        hs = sb("hs", [P, 2, D])
        hTs = sb("hTs", [P, 2, 2, P])
        bsyn_b = sb("bsyn_b", [P, N])
        bout_b = sb("bout_b", [P, D])
        gam_b = sb("gam_b", [P, D])
        bet_b = sb("bet_b", [P, D])
        D_b = sb("D_b", [P, NH])
        ident = sb("ident", [P, P])
        onesf = sb("onesf", [P, P])
        neghalf = sb("neghalf", [P, NT])
        iota9 = sb("iota9", [P, 9])
        gates = sb("gates", [P, 4])
        tg = sb("tg", [P, 4])
        stats = sb("stats", [P, 6])
        mv = sb("mv", [P, NT, 2])
        mvt = sb("mvt", [P, 2])
        rstd = sb("rstd", [P, NT])
        nmr = sb("nmr", [P, NT])
        smax = sb("smax", [P, 2])
        nsmax = sb("nsmax", [P, 2, 2])
        asum = sb("asum", [P, 2, 2])
        rsum = sb("rsum", [P, 2])
        wabs = sb("wabs", [P, 2])
        wsc = sb("wsc", [P, 2])
        wcut = sb("wcut", [P, 2])
        wneg = sb("wneg", [P, 2])
        spread = sb("spread", [P, 2])
        thr = sb("thr", [P, NT])
        nthr = sb("nthr", [P, NT])
        cnt = sb("cnt", [P, NT])
        lo = sb("lo", [P, NT]); clo = sb("clo", [P, NT])
        hi = sb("hi", [P, NT]); chi = sb("chi", [P, NT])
        up = sb("up", [P, NT], u32); dn = sb("dn", [P, NT], u32)
        t1 = sb("t1", [P, NT]); t2 = sb("t2", [P, NT]); t3 = sb("t3", [P, NT])
        m8 = sb("m8", [P, 2, 8])
        m9 = sb("m9", [P, NT, 9])
        m9s = sb("m9s", [P, NT, 9])
        bad = sb("bad", [P, 1])
        bad_i = sb("bad_i", [P, 1], i32)

        H = Z[:, 0:NT * ROW].rearrange("p (t d) -> p t d", t=NT)
        hT = Z[:, 4352:4352 + 2 * T].rearrange("p (k t) -> p k t", k=2)
        back = Z[:, :].rearrange("p (q t d) -> p q t d", q=4, t=NT)
        H2f = H2[:, :, :].rearrange("p t d -> p (t d)")
        shid = H2f[:, 0:1536].rearrange("p (a c t) -> p a c t", a=2, c=3)
        ssil = H2f[:, 1536:3072].rearrange("p (a c t) -> p a c t", a=2, c=3)
        sil0 = H2f[:, 3072:3584].rearrange("p (a t) -> p a t", a=2)
        sil1 = H2f[0:F1, 3584:4096].rearrange("p (a t) -> p a t", a=2)
        qTf = qT[:, :, :, :].rearrange("p l b i -> p (l b i)")
        hid0 = qTf[:, 0:512].rearrange("p (a t) -> p a t", a=2)
        hid1 = qTf[0:F1, 512:1024].rearrange("p (a t) -> p a t", a=2)
        xs_sb = Z[:, 8448:8448 + 8 * ROW].rearrange("p (a b d) -> p a b d", a=4, b=2)
        w_sb = Z[:, 10624:10624 + 4 * (2 * GU + D)].rearrange("p (a f) -> p a f", a=4)
        xT = qTf[:, 2176:2176 + 1024].rearrange("p (a k t) -> p a k t", a=2, k=2)
        wtf = wt[:, :, :].rearrange("p a n -> p (a n)")
        wsgu_sb = wtf[:, 0:2 * 2 * FSH].rearrange("p (k f) -> p k f", k=2)
        wgu_sb = w_sb[:, :, 0:2 * GU].rearrange("p a (k f) -> p a k f", k=2)
        wd0_sb = w_sb[:, :, 2 * GU:2 * GU + D]
        wd1_sb = wtf[0:F1, 1408:1408 + 4 * D].rearrange("p (a d) -> p a d", a=4)
        hidf = hidden[:, :, :].rearrange("p a n -> p (a n)")
        oh = hidf[:, 0:2 * K * E].rearrange("p (q k e) -> p q k e", q=2, k=K)
        prod = hidf[:, 768:768 + 2 * K * E].rearrange("p (q k e) -> p q k e", q=2, k=K)
        hidTf = hidT[:, :, :].rearrange("p a n -> p (a n)")
        y_sb = hidTf.rearrange("p (a b d) -> p a b d", a=4, b=2)
        hst = hidTf[:, 1024:1024 + 4 * D].rearrange("p (a q d) -> p a q d", a=2, q=2)
        fill = sb("fill", [P, 2, ROW])
        wsd_sb = sb("wsd_sb", [P, 3, D])
        gate_sb = sb("gate_sb", [P, 2, E])
        tri = sb("tri", [P, P], bf16)
        trii = sb("trii", [E, E], bf16)
        ones = sb("ones", [P, P], bf16)
        iota_e = sb("iota_e", [P, E])
        iota_row = sb("iota_row", [P, E])
        pid = sb("pid", [P, 1])
        dump = sb("dump", [P, 1])
        lg = sb("lg", [P, 2, E])
        top8 = sb("top8", [P, 2, 8])
        idx8 = sb("idx8", [P, 2, 8], u32)
        idxf = sb("idxf", [P, 2, 8])
        negmax = sb("negmax", [P, 2])
        e64 = sb("e64", [P, 2, E])
        sum64 = sb("sum64", [P, 2])
        e6 = sb("e6", [P, 2, K])
        den = sb("den", [P, 2, 2])
        mask = sb("mask", [P, 2, E], bf16)
        macc = sb("macc", [P, 2, E], bf16)
        msum = sb("msum", [P, E], bf16)
        posr = sb("posr", [P, 2, E])
        slotf = sb("slotf", [P, 2, K])
        slot = sb("slot", [P, NT, K], i32)
        wsel = sb("wsel", [P, 4, 2, K])
        wtok = sb("wtok", [P, 4, 2])
        toki = sb("toki", [P, 4, 2], i32)
        cnt_f = sb("cnt_f", [E, P])
        nb_i = sb("nb_i", [E, P], i32)
        nb_j = sb("nb_j", [E, P], i32)
        nb_b = sb("nb_b", [E, P], bf16)
        ov_s = sb("ov_s", [P, 12])
        ov_w = sb("ov_w", [P, 3, E])
        ov_c = sb("ov_c", [P, 2, E])
        bvals = sb("bvals", [P, 3, P])
        rows_f = sb("rows_f", [P, 3, P])
        gidx = sb("gidx", [P, P], i32)
        gvalid = sb("gvalid", [P, P])
        gpad = sb("gpad", [P, P])
        eb_i = sb("eb_i", [1, 2, P], i32)
        nov_i = sb("nov_i", [P, 1], i32)
        gcol = sb("gcol", [P, 1], i32)
        ovcol = sb("ovcol", [P, 2])
        psum = ctx.enter_context(nc.psum_tensor("psum", [P, 8, 512], f32))
        banks = [psum[:, i, :] for i in range(8)]
        pT, pA, pC, pY = banks[0:2], banks[2:4], banks[4:6], banks[6:8]
        s_banks = [[banks[2], banks[3], banks[4]], [banks[5], banks[0], banks[1]]]

        x_in = sem("x_in")
        small_in = sem("small_in")
        wraw_in = sem("wraw_in")
        consts = sem("consts")
        w_ready = sem("w_ready")
        wabs_ready = sem("wabs_ready")
        wsum_done = sem("wsum_done")
        tg_ready = sem("tg_ready")
        var_ready = sem("var_ready")
        rstd_ready = sem("rstd_ready")
        qn_ready = sem("qn_ready")
        sc_done = sem("sc_done")
        smax_ready = sem("smax_ready")
        attn_ready = sem("attn_ready")
        v_scaled = sem("v_scaled")
        pv_done = sem("pv_done")
        x1_done = sem("x1_done")
        hs_ready = sem("hs_ready")
        hT_full = sem("hT_full")
        hT_ready = sem("hT_ready")
        z_done = sem("z_done")
        z_ready = sem("z_ready")
        h2b_done = sem("h2b_done")
        thr_ready = sem("thr_ready")
        cnt_done = sem("cnt_done")
        masked = sem("masked")
        max_done = sem("max_done")
        bad_ready = sem("bad_ready")
        bad_done = sem("bad_done")
        hid_ready = sem("hid_ready")
        hidT_full = sem("hidT_full")
        hidT_ready = sem("hidT_ready")
        o_done = sem("o_done")
        y0_done = sem("y0_done")
        yn_ready = sem("yn_ready")
        qs_ready = sem("qs_ready")
        qT_full = sem("qT_full")
        qT_ready = sem("qT_ready")
        tdiag_ready = sem("tdiag_ready")
        kv_ready = sem("kv_ready")
        conv_done = sem("conv_done")
        prod_done = sem("prod_done")
        o3_ready = sem("o3_ready")
        o3T_done = sem("o3T_done")
        x3_done = sem("x3_done")
        out_done = sem("out_done")
        v_step = sem("v_step")
        p_step = sem("p_step")
        l_step = sem("l_step")
        gate_in = sem("gate_in")
        ws_in = sem("ws_in")
        xhid_ready = sem("xhid_ready")
        load_done = sem("load_done")
        c_done = sem("c_done")
        filled = sem("filled")
        h_ready = sem("h_ready")
        rT_full = sem("rT_full")
        rT_ready = sem("rT_ready")
        logits_done = sem("logits_done")
        negmax_ready = sem("negmax_ready")
        exp_done = sem("exp_done")
        mask_ready = sem("mask_ready")
        rank_done = sem("rank_done")
        slots_ready = sem("slots_ready")
        scattered = sem("scattered")
        sgu_done = sem("sgu_done")
        ssilu_done = sem("ssilu_done")
        shid_ready = sem("shid_ready")
        sy_done = sem("sy_done")
        base_ready = sem("base_ready")
        xT_full = sem("xT_full")
        xT_ready = sem("xT_ready")
        guA_done = sem("guA_done")
        guC_done = sem("guC_done")
        silA_done = sem("silA_done")
        silC_done = sem("silC_done")
        y_done = sem("y_done")
        y_ready = sem("y_ready")
        tok_ready = sem("tok_ready")
        nb_ready = sem("nb_ready")
        ov_done = sem("ov_done")
        bval_ready = sem("bval_ready")
        brow_done = sem("brow_done")
        ov_ready = sem("ov_ready")
        padded = sem("padded")
        gcol_ready = sem("gcol_ready")
        o_w = sem("o_w")
        o_col = sem("o_col")
        o_tok = sem("o_tok")
        o_x = sem("o_x")
        o_T = sem("o_T")
        o_Tr = sem("o_Tr")
        o_gu = sem("o_gu")
        o_silu = sem("o_silu")
        o_hid = sem("o_hid")
        o_y = sem("o_y")
        o_yr = sem("o_yr")
        o_add = sem("o_add")
        zeroed = sem("zeroed")
        sum_done = sem("sum_done")
        back_in = [sem(f"back_in{c}") for c in range(4)]
        added = [[sem(f"added{q}{j}") for j in range(2)] for q in range(2)]
        w_in = [sem(f"w_in{s}") for s in range(4)]
        xs_in = [sem(f"xs_in{s}") for s in range(4)]
        ctx_in = [sem("ctx_in0"), sem("ctx_in1")]
        head_in = [sem("head_in0"), sem("head_in1")]
        tick = {n: sem("tick_" + n) for n in ("pool", "dve", "sp", "pe", "act")}

        def alone(eng, name):
            eng.sem_inc(tick[name], 1)

        block = ctx.enter_context(nc.Block())

        def bc(ap, n):
            return ap.rearrange("(a n) -> a n", a=1).to_broadcast([P, n])

        @block.sync
        def _(sp):
            for c in range(4):
                sp.dma_start(X[:, 4 * c:4 * c + 4, :], x[4 * c:4 * c + 4].rearrange("b p d -> p b d")).then_inc(x_in, 16)
            sp.dma_start(wraw[:, 0:2, :], wsynT.rearrange("(k p) n -> p k n", p=P)).then_inc(wraw_in, 16)
            sp.dma_start(wraw[:, 2:4, :].rearrange("p a n -> p (a n)").rearrange("p (c d) -> p c d", c=8),
                         woutT.rearrange("(c p) d -> p c d", p=P)).then_inc(wraw_in, 16)

            def load_ctx(b, par):
                sp.dma_start(ctx_s[:, par, :], ctxn[b]).then_inc(ctx_in[par], 16)
                sp.dma_start(ctxT_s[:, par], ctxT[b].rearrange("(k p) s -> p k s", p=P)).then_inc(ctx_in[par], 16)

            load_ctx(0, 0)
            load_ctx(1, 1)
            with sp.Fori(1, NT // 2) as i:
                for par in range(2):
                    b = 2 * i + par
                    sp.wait_ge(sc_done, b - 1)
                    sp.wait_ge(v_scaled, b - 1)
                    alone(sp, "sp")
                    load_ctx(b, par)

            def load_head(h, par):
                sp.dma_start(ctxH_s[:, par].rearrange("p l b i -> p (l b i)"), ctxH[h]).then_inc(head_in[par], 16)
                sp.dma_start(toep_s[:, par].rearrange("p c l -> p (c l)"), toep[h]).then_inc(head_in[par], 16)

            load_head(0, 0)
            load_head(1, 1)
            with sp.Fori(1, NH // 2) as i:
                for par in range(2):
                    h = 2 * i + par
                    sp.wait_ge(kv_ready, h - 1)
                    sp.wait_ge(conv_done, h - 1)
                    alone(sp, "sp")
                    load_head(h, par)

            sp.dma_start(gate_sb[:, :, :], gateT).then_inc(gate_in, 16)
            sp.dma_start(wsd_sb[:, 0:2, :], wsd[0:2 * P, :].rearrange("(c p) d -> p c d", p=P)).then_inc(ws_in, 16)
            sp.dma_start(wsd_sb[0:96, 2, :], wsd[2 * P:FSH, :]).then_inc(ws_in, 16)
            sp.wait_ge(o_done, NT)
            sp.dma_start(wsgu_sb, wsgu).then_inc(ws_in, 16)

            def load_weights(e, s, done):
                sp.dma_start(w_sb[:, s, :], wexp[e]).then_inc(done, 16)
                sp.dma_start(wd1_sb[:, s, :], wd1[e]).then_inc(done, 16)

            def load_rows(e, s):
                sp.dma_start(xs_sb[:, s].rearrange("p b d -> p (b d)"),
                             rows_v[e, 0:CAP, :].rearrange("(p b) d -> p (b d)", b=2)).then_inc(xs_in[s], 16)

            sp.wait_ge(o3_ready, NH)
            for s in range(4):
                load_weights(s, s, w_in[s])
            sp.wait_ge(scattered, 16 * NT * K)
            for s in range(4):
                load_rows(s, s)
            with sp.Fori(1, E // 4) as i:
                for s in range(4):
                    e = 4 * i + s
                    sp.wait_ge(tok_ready, e - 3)
                    sp.wait_ge(y_done, e - 3)
                    load_rows(e, s)
                    load_weights(e, s, w_in[s])
            sp.wait_ge(ov_ready, 1)
            sp.wait_ge(y_ready, E)
            n = sp.value_load(nov_i[0:1, 0:1], min_val=1, max_val=MAXB)
            with sp.Fori(0, n) as b:
                e = sp.value_load(eb_i[0:1, 0, bass.ds(b, 1)], min_val=0, max_val=E - 1)
                row = sp.value_load(eb_i[0:1, 1, bass.ds(b, 1)], min_val=0, max_val=E * T - P)
                sp.wait_ge(o_yr, b + 1)
                alone(sp, "sp")
                sp.dma_start(xs_sb[:, 0, 0, :], xs_rows[bass.ds(row, P), :]).then_inc(o_x, 16)
                load_weights(e, 0, o_w)
            sp.wait_ge(o_yr, n + 1)
            alone(sp, "sp")
            for q in range(2):
                for j in range(2):
                    if (q, j) == (0, 0):
                        sp.wait_ge(o_add, 16 * n)
                        alone(sp, "sp")
                    sp.wait_ge(added[q][j], 16 * (E // 2))
            for c in range(4):
                for q in range(2):
                    for j in range(2):
                        sp.dma_start(back[:, 2 * q + j, 4 * c:4 * c + 4, :],
                                     acc[2 * q + j][c * 4 * P:(c + 1) * 4 * P, :].rearrange("(t p) d -> p t d", p=P)).then_inc(back_in[c], 16)
            for c in range(4):
                sp.wait_ge(sum_done, c + 1)
                sp.dma_start(out[4 * c:4 * c + 4].rearrange("t p d -> p t d"), X[:, 4 * c:4 * c + 4, :]).then_inc(out_done, 16)
            sp.wait_ge(out_done, 64)

        @block.gpsimd
        def _(pool):
            pool.memset(ident[:, :], 0.0)
            pool.memset(onesf[:, :], 1.0)
            pool.memset(neghalf[:, :], -0.5).then_inc(p_step, 1)
            pool.wait_ge(p_step, 1)
            pool.affine_select(out=ident[:, :], in_=ident[:, :], compare_op=ALU.not_equal, fill=1.0,
                               base=0, pattern=[[-1, P]], channel_multiplier=1)
            pool.iota(iota9[:, :], pattern=[[1, 9]], base=0, channel_multiplier=0,
                      allow_small_or_imprecise_dtypes=True).then_inc(consts, 1)

            def pow_half(n):
                pool.wait_ge(var_ready, n)
                pool.tensor_tensor(rstd[:, :], mv[:, :, 1], neghalf[:, :], ALU.pow).then_inc(rstd_ready, 1)

            pool.memset(tri[:, :], 1.0)
            pool.memset(trii[:, :], 1.0)
            pool.memset(ones[:, :], 1.0)
            pool.memset(macc[:, 0, :], 0.0)
            pool.memset(fill[:, :, :], 0.0).then_inc(p_step, 1)
            pool.wait_ge(p_step, 2)
            pool.affine_select(out=tri[:, :], in_=tri[:, :], compare_op=ALU.is_gt, fill=0.0,
                               base=0, pattern=[[1, P]], channel_multiplier=-1)
            pool.affine_select(out=trii[:, :], in_=trii[:, :], compare_op=ALU.is_ge, fill=0.0,
                               base=0, pattern=[[1, E]], channel_multiplier=-1)
            for t_, base, pat, cm in ((iota_e, 0, [[1, E]], 0), (iota_row, 0, [[T, E]], 0), (pid, 0, [[0, 1]], 1),
                                      (dump, E * T, [[0, 1]], 1)):
                pool.iota(t_[:, :], pattern=pat, base=base, channel_multiplier=cm, allow_small_or_imprecise_dtypes=True)
            pow_half(1)
            for a_ in acc:
                for c in range(T // P // 8):
                    pool.dma_start(a_[8 * c * P:8 * (c + 1) * P, :].rearrange("(p r) d -> p r d", r=8),
                                   fill[:, 0:1, 0:D].to_broadcast([P, 8, D])).then_inc(zeroed, 16)
                pool.dma_start(a_[T:T + P, :], fill[:, 0, 0:D]).then_inc(zeroed, 16)
            pool.wait_ge(zeroed, 16 * 12)
            pool.iota(fill[:, :, CT:CT + 1], pattern=[[0, 2], [0, 1]], base=T, channel_multiplier=1,
                      allow_small_or_imprecise_dtypes=True).then_inc(c_done, 1)
            pool.wait_ge(c_done, 1)
            with pool.Fori(0, E) as i:
                pool.dma_start(rows_v[i, 0:CAP, :].rearrange("(p b) d -> p (b d)", b=2),
                               fill[:, :, :].rearrange("p b d -> p (b d)")).then_inc(filled, 16)
            pow_half(2)
            with pool.Fori(0, NT) as b:
                pool.wait_ge(hs_ready, b + 1)
                pool.tensor_tensor(H2[:, b, :], H2[:, b, :], bout_b[:, :], ALU.add)
                pool.tensor_tensor(X[:, b, :], X[:, b, :], bet_b[:, :], ALU.add).then_inc(h2b_done, 1)
            pow_half(3)
            pow_half(4)

            def products(h, par, i, first):
                pool.wait_ge(head_in[par], 32 * i + 32)
                if not first:
                    pool.wait_ge(conv_done, h - 1)
                at = 0
                for d in range(HD):
                    m = pool.tensor_tensor(kv[:, par, :, :, at:at + HD - d], ctxH_s[:, par, :, :, 0:HD - d],
                                           ctxH_s[:, par, :, :, d:HD], ALU.mult)
                    at += HD - d
                m.then_inc(kv_ready, 1)

            pool.wait_ge(hid_ready, NT)
            products(0, 0, 0, True)
            products(1, 1, 0, True)
            with pool.Fori(1, NH // 2) as i:
                products(2 * i, 0, i, False)
                products(2 * i + 1, 1, i, False)

            pool.iota(H[:, :, CT:CT + 1], pattern=[[P, NT], [0, 1]], base=0, channel_multiplier=1, allow_small_or_imprecise_dtypes=True)
            pool.memset(H[:, :, CW + K:ROW], 0.0).then_inc(c_done, 1)
            pow_half(5)
            pool.wait_ge(filled, 16 * E)
            for i in range(NPAIR // 2):
                for par in range(2):
                    u = 2 * i + par
                    pool.wait_ge(slots_ready, u + 1)
                    for q in range(2):
                        for k in range(K):
                            pool.indirect_dma_start(
                                out=xs_rows[:, :],
                                out_offset=bass.IndirectOffsetOnAxis(ap=slot[:, 2 * u + q, k:k + 1], axis=0),
                                in_=H[:, 2 * u + q, :], in_offset=None).then_inc(scattered, 16)
            pool.wait_ge(ov_ready, 1)
            pool.wait_ge(scattered, 16 * NT * K)
            n = pool.value_load(nov_i[0:1, 0:1], min_val=1, max_val=MAXB)
            with pool.Fori(0, n) as b:
                pool.wait_ge(gcol_ready, b + 1)
                alone(pool, "pool")
                pool.indirect_dma_start(out=xs_rows[:, :], out_offset=bass.IndirectOffsetOnAxis(ap=gcol[:, 0:1], axis=0),
                                        in_=fill[:, 0, :], in_offset=None).then_inc(padded, 16)

            def add_rows(i, s, first):
                e, turn = 4 * i + s, 2 * i + s // 2
                pool.wait_ge(y_ready, e + 1)
                alone(pool, "pool")
                for j in range(2):
                    if not (first and s < 2):
                        pool.wait_ge(added[s % 2][j], 16 * turn)
                        alone(pool, "pool")
                    pool.indirect_dma_start(
                        out=acc[2 * (s % 2) + j][:, :], out_offset=bass.IndirectOffsetOnAxis(ap=toki[:, s, j:j + 1], axis=0),
                        in_=y_sb[:, s, j, :], in_offset=None, compute_op=ALU.add).then_inc(added[s % 2][j], 16)

            for s in range(4):
                add_rows(0, s, True)
            with pool.Fori(1, E // 4) as i:
                for s in range(4):
                    add_rows(i, s, False)
            pool.wait_ge(added[0][0], 16 * (E // 2))
            with pool.Fori(0, n) as b:
                pool.wait_ge(o_yr, b + 2)
                alone(pool, "pool")
                pool.indirect_dma_start(
                    out=acc[0][:, :], out_offset=bass.IndirectOffsetOnAxis(ap=toki[:, 0, 0:1], axis=0),
                    in_=y_sb[:, 0, 0, :], in_offset=None, compute_op=ALU.add).then_inc(o_add, 16)
                pool.wait_ge(o_add, 16 * b + 16)
                alone(pool, "pool")

        @block.tensor
        def _(pe):
            pe.wait_ge(consts, 1)
            pe.wait_ge(wabs_ready, 1)
            pe.matmul(psum[:, 7, 0:2], onesf[:, :], wabs[:, :], start=True, stop=True).then_inc(wsum_done, 1)

            def scores(b, par, i, first):
                pe.wait_ge(ctx_in[par], 32 * i + 32)
                pe.wait_ge(qn_ready, b + 1)
                if not first:
                    pe.wait_ge(attn_ready, b - 1)
                for e in range(2):
                    m = pe.matmul(psum[:, par, e * D:(e + 1) * D], ctx_s[:, par, e * P:(e + 1) * P], qn[:, par, :],
                                  start=True, stop=True)
                m.then_inc(sc_done, 1)

            def mix(b, par, first):
                pe.wait_ge(attn_ready, b + 1)
                pe.wait_ge(v_scaled, b + 1)
                if not first:
                    pe.wait_ge(x1_done, b - 1)
                for e in range(2):
                    m = pe.matmul(psum[:, 2 + par, 0:D], vTs[:, par, e, :], attn[:, par, e, :], start=(e == 0), stop=(e == 1))
                m.then_inc(pv_done, 1)

            scores(0, 0, 0, True)
            scores(1, 1, 0, True)
            mix(0, 0, True)
            with pe.Fori(1, NT // 2) as i:
                scores(2 * i, 0, i, False)
                mix(2 * i - 1, 1, False) if False else None
                pe.wait_ge(attn_ready, 2 * i)
                pe.wait_ge(v_scaled, 2 * i)
                for e in range(2):
                    m = pe.matmul(psum[:, 3, 0:D], vTs[:, 1, e, :], attn[:, 1, e, :], start=(e == 0), stop=(e == 1))
                m.then_inc(pv_done, 1)
                scores(2 * i + 1, 1, i, False)
                mix(2 * i, 0, False)
            mix(NT - 1, 1, False)

            def turn(b, par, first):
                pe.wait_ge(hs_ready, b + 1)
                if not first:
                    pe.wait_ge(hT_ready, b - 1)
                for k in range(2):
                    m = pe.transpose(psum[:, par, k * P:(k + 1) * P], hs[:, par, k * P:(k + 1) * P], ident[:, :])
                m.then_inc(hT_full, 1)

            def expand(b, par, first):
                pe.wait_ge(hT_ready, b + 1)
                if not first:
                    pe.wait_ge(z_ready, b - 1)
                for c in range(2):
                    for k in range(2):
                        m = pe.matmul(psum[:, 2 + 2 * par + c, :], hTs[:, par, k, :], wsyn[:, k, c * 512:(c + 1) * 512],
                                      start=(k == 0), stop=(k == 1))
                m.then_inc(z_done, 1)

            pe.wait_ge(w_ready, 1)
            pe.wait_ge(x1_done, NT)
            turn(0, 0, True)
            turn(1, 1, True)
            expand(0, 0, True)
            turn(2, 0, False)
            expand(1, 1, True)
            with pe.Fori(1, NT // 2 - 1) as i:
                turn(2 * i + 1, 1, False)
                expand(2 * i, 0, False)
                turn(2 * i + 2, 0, False)
                expand(2 * i + 1, 1, False)
            turn(NT - 1, 1, False)
            expand(NT - 2, 0, False)
            expand(NT - 1, 1, False)

            pe.wait_ge(bad_ready, 1)
            pe.matmul(psum[:, 0, 0:1], onesf[:, :], bad[:, :], start=True, stop=True).then_inc(bad_done, 1)

            def turn_hidden(b, par, first):
                pe.wait_ge(hid_ready, b + 1)
                if not first:
                    pe.wait_ge(hidT_ready, b - 1)
                for c in range(8):
                    m = pe.transpose(psum[:, 2 + 2 * par + c // 4, (c % 4) * P:(c % 4 + 1) * P],
                                     hidden[:, par, c * P:(c + 1) * P], ident[:, :])
                m.then_inc(hidT_full, 1)

            def project(b, par, first):
                pe.wait_ge(hidT_ready, b + 1)
                if not first:
                    pe.wait_ge(y0_done, b - 1)
                for c in range(8):
                    m = pe.matmul(psum[:, par, 0:D], hidT[:, par, c * P:(c + 1) * P], wout[:, c, :], start=(c == 0), stop=(c == 7))
                m.then_inc(o_done, 1)

            turn_hidden(0, 0, True)
            turn_hidden(1, 1, True)
            project(0, 0, True)
            turn_hidden(2, 0, False)
            project(1, 1, True)
            with pe.Fori(1, NT // 2 - 1) as i:
                turn_hidden(2 * i + 1, 1, False)
                project(2 * i, 0, False)
                turn_hidden(2 * i + 2, 0, False)
                project(2 * i + 1, 1, False)
            turn_hidden(NT - 1, 1, False)
            project(NT - 2, 0, False)
            project(NT - 1, 1, False)

            pe.wait_ge(y0_done, NT)

            def turn_q(b, par, first):
                pe.wait_ge(qs_ready, b + 1)
                if not first:
                    pe.wait_ge(qT_ready, b - 1)
                for k in range(2):
                    m = pe.transpose(psum[:, par, k * P:(k + 1) * P], hs[:, par, k * P:(k + 1) * P], ident[:, :])
                m.then_inc(qT_full, 1)

            turn_q(0, 0, True)
            turn_q(1, 1, True)
            with pe.Fori(1, NT // 2) as i:
                turn_q(2 * i, 0, False)
                turn_q(2 * i + 1, 1, False)
            pe.wait_ge(qT_ready, NT)

            def conv(h, par, first):
                pe.wait_ge(kv_ready, h + 1)
                pe.wait_ge(tdiag_ready, h + 1)
                if not first:
                    pe.wait_ge(prod_done, h - 1)
                for g in range(2):
                    r = [kv[:, par, m_, 8 * g:8 * g + 8, :].rearrange("p b r -> p (b r)") for m_ in range(2)]
                    w = 8 * NPR
                    pe.matmul(psum[:, 4 * par + g, 0:w], tdiag[:, par, :], r[0], start=True, stop=True)
                    pe.matmul(psum[:, 4 * par + 2 + g, 0:w], toep_s[:, par, 1, :], r[0], start=True, stop=False)
                    m = pe.matmul(psum[:, 4 * par + 2 + g, 0:w], tdiag[:, par, :], r[1], start=False, stop=True)
                m.then_inc(conv_done, 1)

            conv(0, 0, True)
            conv(1, 1, True)
            with pe.Fori(1, NH // 2) as i:
                conv(2 * i, 0, False)
                conv(2 * i + 1, 1, False)

            pe.wait_ge(o3_ready, NH)
            for b in range(NT):
                if b >= 4:
                    pe.wait_ge(x3_done, b - 3)
                for l in range(2):
                    m = pe.transpose(psum[:, b % 4, l * P:(l + 1) * P], OT[:, l, b, :], ident[:, :])
                m.then_inc(o3T_done, 1)

            pe.wait_ge(x3_done, NT)
            pe.wait_ge(gate_in, 16)

            def rank_tile(par, q):
                o = pY[par][:, E * q:E * q + E]
                pe.matmul(o, tri[:, :], mask[:, q, :], start=True, stop=False)
                if q == 1:
                    pe.matmul(o, ones[:, :], mask[:, 0, :], start=False, stop=False)
                return pe.matmul(o, ones[:, :], macc[:, par, :], start=False, stop=True)

            with pe.Fori(0, NPAIR // 2) as i:
                for par in range(2):
                    u = 2 * i + par
                    pe.wait_ge(h_ready, u + 1)
                    for q in range(2):
                        for k in range(2):
                            m = pe.transpose(pT[par][:, k * CAP + q * P:k * CAP + (q + 1) * P],
                                             hst[:, par, q, k * P:(k + 1) * P], ident[:, :])
                    m.then_inc(rT_full, 1)
                    pe.wait_ge(rT_ready, u + 1)
                    for q in range(2):
                        for k in range(2):
                            m = pe.matmul(pA[par][:, E * q:E * q + E], xT[:, par, k, q * P:(q + 1) * P],
                                          gate_sb[:, k, :], start=(k == 0), stop=(k == 1))
                    m.then_inc(logits_done, 1)
                    pe.wait_ge(mask_ready, u + 1)
                    rank_tile(par, 0)
                    rank_tile(par, 1).then_inc(rank_done, 1)

            pe.wait_ge(slots_ready, NPAIR)
            pe.matmul(pT[0][0:E, 0:P], macc[:, 0, :], ones[:, :], start=True, stop=True)
            pe.matmul(pT[0][:, P:P + E], ones[:, :], macc[:, 0, :], start=True, stop=True).then_inc(load_done, 1)
            pe.wait_ge(nb_ready, 1)
            pe.matmul(pT[1][:, 0:E], nb_b[:, :], trii[:, :], start=True, stop=True)
            pe.matmul(pT[1][:, E:2 * E], nb_b[:, :], tri[0:E, 0:E], start=True, stop=True).then_inc(ov_done, 1)
            pe.wait_ge(bval_ready, 1)
            for v in range(3):
                m = pe.matmul(pY[0][:, v * P:(v + 1) * P], bvals[:, v, :], ident[:, :], start=True, stop=True)
            m.then_inc(brow_done, 1)
            pe.wait_ge(ov_ready, 1)

            pe.wait_ge(ws_in, 48)

            def shared_up(u, par, first):
                if not first:
                    pe.wait_ge(shid_ready, 3 * u - 3)
                for c, (f0, fw) in enumerate(FS):
                    for g in range(2):
                        for k in range(2):
                            m = pe.matmul(s_banks[par][c][0:fw, g * CAP:(g + 1) * CAP],
                                          wsgu_sb[:, k, g * FSH + f0:g * FSH + f0 + fw],
                                          hT[:, k, bass.ds(u * CAP, CAP)], start=(k == 0), stop=(k == 1))
                    m.then_inc(sgu_done, 1)

            def shared_down(u, par, first):
                pe.wait_ge(shid_ready, 3 * u + 3)
                if not first:
                    pe.wait_ge(base_ready, u - 1)
                for j in range(2):
                    for c, (f0, fw) in enumerate(FS):
                        m = pe.matmul(pY[par][:, j * D:(j + 1) * D], shid[0:fw, par, c, j * P:(j + 1) * P],
                                      wsd_sb[0:fw, c, :], start=(c == 0), stop=(c == 2))
                m.then_inc(sy_done, 1)

            shared_up(0, 0, True)
            shared_up(1, 1, True)
            shared_down(0, 0, True)
            with pe.Fori(1, NPAIR // 2) as i:
                shared_up(2 * i, 0, False)
                pe.wait_ge(sy_done, 2 * i - 1)
                shared_down(2 * i - 1, 1, False)
                shared_up(2 * i + 1, 1, False)
                shared_down(2 * i, 0, False)
            shared_down(NPAIR - 1, 1, False)

            def transposes(i, s, first):
                e, par = 4 * i + s, s % 2
                pe.wait_ge(xs_in[s], 16 * i + 16)
                if not first:
                    pe.wait_ge(xT_ready, e - 1)
                for j in range(2):
                    for k in range(2):
                        m = pe.transpose(pT[par][:, k * CAP + j * P:k * CAP + (j + 1) * P],
                                         xs_sb[:, s, j, k * P:(k + 1) * P], ident[:, :])
                m.then_inc(xT_full, 1)

            def up(i, s, first):
                e, par = 4 * i + s, s % 2
                pe.wait_ge(w_in[s], 32 * i + 32)
                pe.wait_ge(xT_ready, e + 1)
                if not first:
                    pe.wait_ge(xhid_ready, e - 1)
                for g in range(2):
                    for k in range(2):
                        m = pe.matmul(pA[par][:, g * CAP:(g + 1) * CAP], wgu_sb[:, s, k, g * P:(g + 1) * P],
                                      xT[:, par, k, :], start=(k == 0), stop=(k == 1))
                m.then_inc(guA_done, 1)
                for k in range(2):
                    m = pe.matmul(pC[par][0:GU - 2 * P, 0:CAP], wgu_sb[:, s, k, 2 * P:GU],
                                  xT[:, par, k, :], start=(k == 0), stop=(k == 1))
                m.then_inc(guC_done, 1)

            def down(i, s):
                e, par = 4 * i + s, s % 2
                pe.wait_ge(xhid_ready, e + 1)
                for j in range(2):
                    pe.matmul(pY[par][:, j * D:(j + 1) * D], hid0[:, par, j * P:(j + 1) * P],
                              wd0_sb[:, s, :], start=True, stop=False)
                    m = pe.matmul(pY[par][:, j * D:(j + 1) * D], hid1[:, par, j * P:(j + 1) * P],
                                  wd1_sb[:, s, :], start=False, stop=True)
                m.then_inc(y_done, 1)

            pe.wait_ge(base_ready, NPAIR)
            transposes(0, 0, True)
            transposes(0, 1, True)
            up(0, 0, True)
            transposes(0, 2, False)
            up(0, 1, True)
            down(0, 0)
            transposes(0, 3, False)
            up(0, 2, False)
            down(0, 1)
            with pe.Fori(1, E // 4) as i:
                for s in range(4):
                    transposes(i, s, False)
                    up(i - (s == 0), (s - 1) % 4, False)
                    down(i - (s < 2), (s - 2) % 4)
            up(E // 4 - 1, 3, False)
            down(E // 4 - 1, 2)
            down(E // 4 - 1, 3)

            n = pe.value_load(nov_i[0:1, 0:1], min_val=1, max_val=MAXB)
            with pe.Fori(0, n) as b:
                pe.wait_ge(o_x, 16 * b + 16)
                for k in range(2):
                    m = pe.transpose(pT[0][:, k * P:(k + 1) * P], xs_sb[:, 0, 0, k * P:(k + 1) * P], ident[:, :])
                m.then_inc(o_T, 1)
                pe.wait_ge(o_w, 32 * b + 32)
                pe.wait_ge(o_Tr, b + 1)
                for g in range(2):
                    for k in range(2):
                        pe.matmul(pA[0][:, g * P:(g + 1) * P], wgu_sb[:, 0, k, g * P:(g + 1) * P],
                                  xT[:, 0, k, 0:P], start=(k == 0), stop=(k == 1))
                for k in range(2):
                    m = pe.matmul(pC[0][0:GU - 2 * P, 0:P], wgu_sb[:, 0, k, 2 * P:GU],
                                  xT[:, 0, k, 0:P], start=(k == 0), stop=(k == 1))
                m.then_inc(o_gu, 1)
                pe.wait_ge(o_hid, b + 1)
                pe.matmul(pY[0][:, 0:D], hid0[:, 0, 0:P], wd0_sb[:, 0, :], start=True, stop=False)
                pe.matmul(pY[0][:, 0:D], hid1[:, 0, 0:P], wd1_sb[:, 0, :], start=False, stop=True).then_inc(o_y, 1)

        @block.scalar
        def _(act):
            for dst, src, n in ((gates, gates_in, 4), (bsyn_b, bsyn, N), (bout_b, bout, D), (gam_b, gamma, D),
                                (bet_b, beta, D), (D_b, ssm_D, NH)):
                act.dma_start(dst[:, :], bc(src, n)).then_inc(small_in, 16)
            act.wait_ge(small_in, 96)
            act.activation(tg[:, :], gates[:, :], ACT.Tanh).then_inc(tg_ready, 1)

            def soft(b, par, first):
                act.wait_ge(smax_ready, b + 1)
                if not first:
                    act.wait_ge(pv_done, b - 1)
                for e in range(2):
                    m = act.activation(attn[:, par, e, :], psum[:, par, e * D:(e + 1) * D], ACT.Exp,
                                       bias=nsmax[:, par, e:e + 1], scale=1.0 / 16, accum_out=asum[:, par, e:e + 1])
                m.then_inc(attn_ready, 1)

            soft(0, 0, True)
            soft(1, 1, True)
            with act.Fori(1, NT // 2) as i:
                soft(2 * i, 0, False)
                soft(2 * i + 1, 1, False)

            def evac_h(b, par, first):
                act.wait_ge(hT_full, b + 1)
                if not first:
                    act.wait_ge(z_done, b - 1)
                act.activation(hTs[:, par], psum[:, par, 0:D].rearrange("p (k c) -> p k c", k=2), ACT.Copy).then_inc(hT_ready, 1)

            evac_h(0, 0, True)
            evac_h(1, 1, True)
            with act.Fori(1, NT // 2) as i:
                evac_h(2 * i, 0, False)
                evac_h(2 * i + 1, 1, False)

            act.wait_ge(z_ready, NT)
            for r in range(ROUNDS):
                act.wait_ge(thr_ready, r + 1)
                with act.Fori(NTD, NT) as t:
                    m = act.activation(hidT[:, 0, :], z[:, t, :], ACT.Sign, bias=nthr[:, bass.ds(t, 1)],
                                       accum_out=cnt[:, bass.ds(t, 1)])
                    m.then_inc(cnt_done, 1)
                    act.wait_ge(cnt_done, (NT - NTD) * r - NTD + 1 + t)

            def evac_hidden(b, par, first):
                act.wait_ge(hidT_full, b + 1)
                if not first:
                    act.wait_ge(o_done, b - 1)
                act.activation(hidT[:, par, :].rearrange("p (a n) -> p a n", a=2), psum[:, 2 + 2 * par:4 + 2 * par, :],
                               ACT.Copy).then_inc(hidT_ready, 1)

            evac_hidden(0, 0, True)
            evac_hidden(1, 1, True)
            with act.Fori(1, NT // 2) as i:
                evac_hidden(2 * i, 0, False)
                evac_hidden(2 * i + 1, 1, False)

            act.wait_ge(yn_ready, 1)
            with act.Fori(0, NT) as t:
                act.activation(H2[:, t, :], H2[:, t, :], ACT.Identity, bias=nmr[:, bass.ds(t, 1)],
                               scale=rstd[:, bass.ds(t, 1)]).then_inc(yn_ready, 1)

            def evac_q(b, par):
                act.wait_ge(qT_full, b + 1)
                act.activation(qT[:, :, b, :], psum[:, par, 0:D].rearrange("p (k c) -> p k c", k=2), ACT.Copy).then_inc(qT_ready, 1)

            with act.Fori(0, NT // 2) as i:
                evac_q(2 * i, 0)
                evac_q(2 * i + 1, 1)

            with act.Fori(0, NPAIR // 2) as i:
                for par in range(2):
                    u = 2 * i + par
                    act.wait_ge(rT_full, u + 1)
                    pv = pT[par][:, :].rearrange("p (k c) -> p k c", k=2)
                    act.activation(xT[:, par], pv, ACT.Copy).then_inc(rT_ready, 1)
                    act.activation(hT[:, :, bass.ds(u * CAP, CAP)], pv, ACT.Copy)
                    act.wait_ge(negmax_ready, u + 1)
                    for q in range(2):
                        act.activation(e64[:, q], lg[:, q], ACT.Exp, bias=negmax[:, q:q + 1],
                                       accum_out=sum64[:, q:q + 1])
                        m = act.activation(e6[:, q], top8[:, q, 0:K], ACT.Exp, bias=negmax[:, q:q + 1])
                    m.then_inc(exp_done, 1)
            with act.Fori(0, NPAIR // 2) as i:
                for par in range(2):
                    u = 2 * i + par
                    for c, (f0, fw) in enumerate(FS):
                        act.wait_ge(sgu_done, 3 * u + c + 1)
                        act.activation(ssil[0:fw, par, c], s_banks[par][c][0:fw, 0:CAP], ACT.Silu).then_inc(ssilu_done, 1)

            def evac(e, par, first):
                act.wait_ge(xT_full, e + 1)
                if not first:
                    act.wait_ge(guC_done, e - 1)
                act.activation(xT[:, par], pT[par][:, :].rearrange("p (k c) -> p k c", k=2), ACT.Copy).then_inc(xT_ready, 1)

            def silu(e, par, first):
                act.wait_ge(guA_done, e + 1)
                if not first:
                    act.wait_ge(xhid_ready, e - 1)
                act.activation(sil0[:, par], pA[par][:, 0:CAP], ACT.Silu).then_inc(silA_done, 1)
                act.wait_ge(guC_done, e + 1)
                act.activation(sil1[:, par], pC[par][0:F1, 0:CAP], ACT.Silu).then_inc(silC_done, 1)

            evac(0, 0, True)
            evac(1, 1, True)
            silu(0, 0, True)
            evac(2, 0, False)
            silu(1, 1, True)
            evac(3, 1, False)
            silu(2, 0, False)
            with act.Fori(1, E // 2 - 1) as i:
                evac(2 * i + 2, 0, False)
                silu(2 * i + 1, 1, False)
                evac(2 * i + 3, 1, False)
                silu(2 * i + 2, 0, False)
            silu(E - 1, 1, False)
            act.wait_ge(ov_ready, 1)
            n = act.value_load(nov_i[0:1, 0:1], min_val=1, max_val=MAXB)
            with act.Fori(0, n) as b:
                act.wait_ge(o_T, b + 1)
                act.activation(xT[:, 0, :, 0:P], pT[0][:, 0:CAP].rearrange("p (k c) -> p k c", k=2), ACT.Copy).then_inc(o_Tr, 1)
                act.wait_ge(o_gu, b + 1)
                act.activation(sil0[:, 0, 0:P], pA[0][:, 0:P], ACT.Silu)
                act.activation(sil1[:, 0, 0:P], pC[0][0:F1, 0:P], ACT.Silu).then_inc(o_silu, 1)

        @block.vector
        def _(dve):
            v = {"at": 0, "k": 0}

            def link(ins):
                v["k"] += 1
                ins.then_inc(v_step, 1)
                dve.wait_ge(v_step, v["at"] + v["k"])

            def loop_in(i0, per):
                v["save"] = v["at"] + v["k"]
                return v["save"]

            def tiles(lo_, hi_, per, body):
                start = v["at"] + v["k"]
                with dve.Fori(lo_, hi_) as i:
                    v["at"], v["k"] = start + (i - lo_) * per, 0
                    body(i)
                    assert v["k"] == per, (v["k"], per)
                v["at"], v["k"] = start + (hi_ - lo_) * per, 0

            def moments(src, t, signal=None):
                alone(dve, "dve")
                link(dve.bn_stats(stats[:, :], src))
                alone(dve, "dve")
                link(dve.bn_aggr(mvt[:, :], stats[:, :]))
                m = dve.tensor_copy(mv[:, t, :], mvt[:, :])
                if signal:
                    m.then_inc(signal, 1)
                else:
                    link(m)

            def variance(n):
                dve.tensor_scalar(mv[:, :, 1], mv[:, :, 1], 1e-5, None, ALU.add).then_inc(var_ready, 1)

            dve.wait_ge(x_in, 64)
            tiles(0, NT, 3, lambda t: moments(X[:, t, :], t))
            variance(1)
            dve.wait_ge(wraw_in, 32)
            dve.tensor_reduce(wabs[:, 0:1], wraw[:, 0:2, :], AX.XY, ALU.add, apply_absolute_value=True)
            dve.tensor_reduce(wabs[:, 1:2], wraw[:, 2:4, :], AX.XY, ALU.add, apply_absolute_value=True).then_inc(wabs_ready, 1)
            dve.wait_ge(wsum_done, 1)
            link(dve.tensor_scalar(wsc[:, :], psum[:, 7, 0:2], 1.0 / (D * N), None, ALU.mult))
            link(dve.tensor_scalar(wcut[:, :], wsc[:, :], 1e-8, 0.5, ALU.add, ALU.mult))
            link(dve.tensor_scalar(wneg[:, :], wcut[:, :], -1.0, None, ALU.mult))
            for w in range(2):
                link(dve.tensor_scalar(wt[:, 2 * w:2 * w + 2, :], wraw[:, 2 * w:2 * w + 2, :], wneg[:, w:w + 1], None, ALU.is_lt))
                m = dve.scalar_tensor_tensor(wt[:, 2 * w:2 * w + 2, :], wraw[:, 2 * w:2 * w + 2, :], wcut[:, w:w + 1],
                                             wt[:, 2 * w:2 * w + 2, :], ALU.is_gt, ALU.subtract)
            m.then_inc(w_ready, 1)
            dve.wait_ge(small_in, 96)
            dve.wait_ge(tg_ready, 1)
            dve.tensor_scalar(gam_b[:, :], gam_b[:, :], tg[:, 1:2], None, ALU.mult)
            dve.tensor_scalar(bet_b[:, :], bet_b[:, :], tg[:, 1:2], None, ALU.mult)
            link(dve.tensor_scalar(spread[:, 0:1], wsc[:, 0:1], SIG, None, ALU.mult))
            dve.tensor_scalar(spread[:, 1:2], spread[:, 0:1], 1.0 / DENS, None, ALU.mult)
            dve.wait_ge(rstd_ready, 1)
            dve.wait_ge(consts, 1)

            def query(b, par, first):
                if not first:
                    dve.wait_ge(sc_done, b - 1)
                dve.tensor_scalar(qn[:, par, :], X[:, b, :], mv[:, b, 0:1], rstd[:, bass.ds(b, 1)], ALU.subtract, ALU.mult).then_inc(qn_ready, 1)

            def highest(b, par):
                dve.wait_ge(sc_done, b + 1)
                link(dve.tensor_reduce(smax[:, :], psum[:, par, :].rearrange("p (e d) -> p e d", e=2), AX.X, ALU.max))
                dve.tensor_scalar(nsmax[:, par, :], smax[:, :], -1.0 / 16, None, ALU.mult).then_inc(smax_ready, 1)

            def scale_v(b, par, i):
                dve.wait_ge(attn_ready, b + 1)
                dve.wait_ge(ctx_in[par], 32 * i + 32)
                link(dve.reciprocal(rsum[:, :], asum[:, par, :]))
                for e in range(2):
                    m = dve.tensor_scalar(vTs[:, par, e, :], ctxT_s[:, par, e, :], rsum[:, e:e + 1], None, ALU.mult)
                m.then_inc(v_scaled, 1)

            def add1(b, par):
                dve.wait_ge(pv_done, b + 1)
                m = dve.scalar_tensor_tensor(X[:, b, :], psum[:, 2 + par, 0:D], tg[:, 0:1], X[:, b, :], ALU.mult, ALU.add)
                m.then_inc(x1_done, 1)
                dve.wait_ge(x1_done, b + 1)

            query(0, 0, True)
            query(1, 1, True)
            highest(0, 0)
            scale_v(0, 0, 0)
            query(2, 0, False)
            highest(1, 1)
            add1(0, 0)
            moments(X[:, 0, :], 0)
            scale_v(1, 1, 0)
            query(3, 1, False)

            def first_pair(i):
                for par in range(2):
                    b = 2 * i + par
                    highest(b, par)
                    add1(b - 1, 1 - par)
                    moments(X[:, b - 1, :], b - 1)
                    scale_v(b, par, i)
                    query(b + 2, par, False)

            tiles(1, NT // 2 - 1, 10, first_pair)
            for par in range(2):
                b = NT - 2 + par
                highest(b, par)
                add1(b - 1, 1 - par)
                moments(X[:, b - 1, :], b - 1)
                scale_v(b, par, NT // 2 - 1)
            add1(NT - 1, 1)
            moments(X[:, NT - 1, :], NT - 1)
            variance(2)
            dve.wait_ge(rstd_ready, 2)

            def norm_h(b, par, first):
                if not first:
                    dve.wait_ge(hT_full, b - 1)
                dve.tensor_scalar(hs[:, par, :], X[:, b, :], mv[:, b, 0:1], rstd[:, bass.ds(b, 1)], ALU.subtract, ALU.mult)
                dve.tensor_scalar(H2[:, b, :], X[:, b, :], mv[:, b, 0:1], rstd[:, bass.ds(b, 1)], ALU.subtract, ALU.mult).then_inc(hs_ready, 1)

            def keep_z(b, par):
                dve.wait_ge(z_done, b + 1)
                dve.scalar_tensor_tensor(z[:, b, :].rearrange("p (a n) -> p a n", a=2), psum[:, 2 + 2 * par:4 + 2 * par, :], wsc[:, 0:1],
                                         bsyn_b[:, :].rearrange("p (a n) -> p a n", a=2), ALU.mult, ALU.add).then_inc(z_ready, 1)

            norm_h(0, 0, True)
            norm_h(1, 1, True)
            norm_h(2, 0, False)
            keep_z(0, 0)

            def z_pair(i):
                norm_h(2 * i + 1, 1, False)
                keep_z(2 * i - 1, 1)
                norm_h(2 * i + 2, 0, False)
                keep_z(2 * i, 0)

            tiles(1, NT // 2 - 1, 0, z_pair)
            norm_h(NT - 1, 1, False)
            keep_z(NT - 3, 1)
            keep_z(NT - 2, 0)
            keep_z(NT - 1, 1)
            dve.wait_ge(z_ready, NT)

            dve.tensor_scalar(thr[:, :], ident[:, 0:NT], 0.0, spread[:, 0:1], ALU.mult, ALU.add) if False else None
            link(dve.memset(thr[:, :], 1.2817))
            link(dve.tensor_scalar(thr[:, :], thr[:, :], spread[:, 0:1], None, ALU.mult))
            dve.tensor_scalar(nthr[:, :], thr[:, :], -1.0, None, ALU.mult).then_inc(thr_ready, 1)

            def count(t, at):
                return dve.tensor_scalar(hidden[:, 0, :], z[:, t, :], at[:, bass.ds(t, 1)], 0.0, ALU.is_ge, ALU.add,
                                         accum_out=cnt[:, bass.ds(t, 1)])

            for r in range(ROUNDS):
                with dve.Fori(0, NTD) as t:
                    count(t, thr).then_inc(l_step, 1)
                    dve.wait_ge(l_step, NTD * r + t + 1)
                    alone(dve, "dve")
                dve.wait_ge(cnt_done, (NT - NTD) * (r + 1))
                link(dve.tensor_scalar(cnt[:, NTD:NT], cnt[:, NTD:NT], 0.5, N / 2.0, ALU.mult, ALU.add))
                dve.tensor_scalar(up[:, :], cnt[:, :], float(TOPK), None, ALU.is_gt)
                dve.tensor_scalar(dn[:, :], cnt[:, :], float(TOPK), None, ALU.is_le)
                if r == 0:
                    link(dve.tensor_scalar(t1[:, :], cnt[:, :], FAR - AIM, spread[:, 1:2], ALU.add, ALU.mult))
                    link(dve.tensor_scalar(t2[:, :], cnt[:, :], -FAR - AIM, spread[:, 1:2], ALU.add, ALU.mult))
                    dve.tensor_tensor(hi[:, :], thr[:, :], t1[:, :], ALU.add)
                    dve.tensor_tensor(lo[:, :], thr[:, :], t2[:, :], ALU.add)
                    dve.memset(chi[:, :], AIM - FAR)
                    link(dve.memset(clo[:, :], AIM + FAR))
                else:
                    link(dve.tensor_copy(t1[:, :], thr[:, :]))
                dve.copy_predicated(lo[:, :], up[:, :], thr[:, :])
                dve.copy_predicated(clo[:, :], up[:, :], cnt[:, :])
                dve.copy_predicated(hi[:, :], dn[:, :], thr[:, :])
                link(dve.copy_predicated(chi[:, :], dn[:, :], cnt[:, :]))
                if r < ROUNDS - 1:
                    dve.tensor_tensor(t1[:, :], clo[:, :], chi[:, :], ALU.subtract)
                    dve.tensor_tensor(t2[:, :], hi[:, :], lo[:, :], ALU.subtract)
                    link(dve.tensor_scalar(t3[:, :], clo[:, :], -float(AIM), None, ALU.add))
                    link(dve.reciprocal(t1[:, :], t1[:, :]))
                    link(dve.tensor_tensor(t2[:, :], t2[:, :], t3[:, :], ALU.mult))
                    link(dve.tensor_tensor(t2[:, :], t2[:, :], t1[:, :], ALU.mult))
                    link(dve.tensor_tensor(t2[:, :], t2[:, :], lo[:, :], ALU.add))
                    link(dve.tensor_tensor(t2[:, :], t2[:, :], hi[:, :], ALU.min))
                    link(dve.tensor_tensor(thr[:, :], t2[:, :], lo[:, :], ALU.max))
                    dve.tensor_scalar(nthr[:, :], thr[:, :], -1.0, None, ALU.mult).then_inc(thr_ready, 1)
                else:
                    link(dve.tensor_copy(m9[:, :, 0], hi[:, :]))
                    dve.tensor_copy(thr[:, :], hi[:, :]).then_inc(thr_ready, 1)
            with dve.Fori(NTD, NT) as t:
                dve.tensor_scalar(z[:, t, :] if False else hidT[:, 1, :], z[:, t, :], hi[:, bass.ds(t, 1)], 0.0, ALU.is_ge, ALU.add,
                                  accum_out=chi[:, bass.ds(t, 1)]).then_inc(l_step, 1)
                dve.wait_ge(l_step, NTD * (ROUNDS - 1) + t + 1)
                alone(dve, "dve")

            def keep_max(i):
                for par in range(2):
                    t = 2 * i + par
                    dve.scalar_tensor_tensor(hidden[:, par, :], z[:, t, :], hi[:, bass.ds(t, 1)], z[:, t, :],
                                             ALU.is_lt, ALU.mult).then_inc(masked, 1)
                    dve.wait_ge(masked, t + 1)
                    alone(dve, "dve")
                    m = dve.max(m8[:, par, :], hidden[:, par, :])
                    m.then_inc(max_done, 1)
                    dve.wait_ge(max_done, t + 1)
                    dve.tensor_copy(m9[:, t, 1:9], m8[:, par, :])

            tiles(0, NT // 2, 0, keep_max)
            dve.tensor_scalar(t1[:, :], chi[:, :], -1.0, float(TOPK), ALU.mult, ALU.add)
            dve.tensor_scalar(t2[:, :], chi[:, :], float(NEAR), None, ALU.is_ge)
            link(dve.tensor_scalar(t3[:, :], chi[:, :], float(TOPK), None, ALU.is_le))
            link(dve.tensor_tensor(t2[:, :], t2[:, :], t3[:, :], ALU.mult))
            link(dve.tensor_reduce(bad[:, :], t2[:, :], AX.X, ALU.min))
            link(dve.tensor_scalar(bad[:, :], bad[:, :], -1.0, 1.0, ALU.mult, ALU.add))
            dve.tensor_copy(bad[:, :], bad[:, :]).then_inc(bad_ready, 1)
            link(dve.tensor_tensor(m9s[:, :, :], iota9[:, None, :].to_broadcast([P, NT, 9]), t1[:, :, None].to_broadcast([P, NT, 9]), ALU.is_equal))
            link(dve.tensor_tensor(m9s[:, :, :], m9s[:, :, :], m9[:, :, :], ALU.mult))
            link(dve.tensor_reduce(thr[:, :], m9s[:, :, :], AX.X, ALU.add))
            dve.wait_ge(bad_done, 1)
            link(dve.tensor_copy(bad_i[:, :], psum[:, 0, 0:1]))
            n_bad = dve.value_load(bad_i[0:1, 0:1], min_val=0, max_val=P)
            with dve.If(n_bad > 0):
                with dve.Fori(0, NT) as t:
                    steps = 2 * ((TOPK - 1) // 8) + 2
                    k = 1
                    dve.tensor_copy(hidden[:, 0, :], z[:, t, :]).then_inc(p_step, 1)
                    dve.wait_ge(p_step, 2 + t * steps + k)
                    for q in range((TOPK - 1) // 8):
                        alone(dve, "dve")
                        dve.max(m8[:, 0, :], hidden[:, 0, :]).then_inc(p_step, 1)
                        k += 1
                        dve.wait_ge(p_step, 2 + t * steps + k)
                        alone(dve, "dve")
                        dve.match_replace(hidden[:, 0, :], m8[:, 0, :], hidden[:, 0, :], -3e38).then_inc(p_step, 1)
                        k += 1
                        dve.wait_ge(p_step, 2 + t * steps + k)
                    alone(dve, "dve")
                    dve.max(m8[:, 0, :], hidden[:, 0, :]).then_inc(p_step, 1)
                    k += 1
                    assert k == steps
                    dve.wait_ge(p_step, 2 + t * steps + k)
                    dve.tensor_copy(thr[:, bass.ds(t, 1)], m8[:, 0, (TOPK - 1) % 8:(TOPK - 1) % 8 + 1])
                dve.memset(t1[:, :], 0.0)
            dve.memset(t1[:, :], 0.0)
            link(dve.tensor_scalar(thr[:, :], thr[:, :], 0.0, None, ALU.max))

            def make_hidden(b, par, first):
                if not first:
                    dve.wait_ge(hidT_full, b - 1)
                dve.scalar_tensor_tensor(hidden[:, par, :], z[:, b, :], thr[:, bass.ds(b, 1)], z[:, b, :], ALU.is_ge, ALU.mult).then_inc(hid_ready, 1)

            def residual(b, par):
                dve.wait_ge(o_done, b + 1)
                dve.wait_ge(h2b_done, b + 1)
                link(dve.scalar_tensor_tensor(H2[:, b, :], psum[:, par, 0:D], wsc[:, 1:2], H2[:, b, :], ALU.mult, ALU.add))
                moments(H2[:, b, :], b, y0_done)

            make_hidden(0, 0, True)
            make_hidden(1, 1, True)
            make_hidden(2, 0, False)
            residual(0, 0)

            def hid_pair(i):
                make_hidden(2 * i + 1, 1, False)
                residual(2 * i - 1, 1)
                make_hidden(2 * i + 2, 0, False)
                residual(2 * i, 0)

            tiles(1, NT // 2 - 1, 6, hid_pair)
            make_hidden(NT - 1, 1, False)
            residual(NT - 3, 1)
            residual(NT - 2, 0)
            residual(NT - 1, 1)
            dve.wait_ge(y0_done, NT)
            variance(3)
            dve.wait_ge(rstd_ready, 3)
            dve.scalar_tensor_tensor(nmr[:, :], mv[:, :, 0], -1.0, rstd[:, :], ALU.mult, ALU.mult).then_inc(yn_ready, 1)

            def add2(t):
                dve.wait_ge(yn_ready, t + 2)
                link(dve.tensor_tensor(H2[:, t, :], H2[:, t, :], gam_b[:, :], ALU.mult))
                link(dve.tensor_tensor(X[:, t, :], X[:, t, :], H2[:, t, :], ALU.add))
                moments(X[:, t, :], t)

            tiles(0, NT, 5, add2)
            variance(4)
            dve.wait_ge(rstd_ready, 4)

            def query3(b, par, first):
                if not first:
                    dve.wait_ge(qT_full, b - 1)
                dve.tensor_scalar(hs[:, par, :], X[:, b, :], mv[:, b, 0:1], rstd[:, bass.ds(b, 1)], ALU.subtract, ALU.mult).then_inc(qs_ready, 1)

            query3(0, 0, True)
            query3(1, 1, True)

            def q_pair(i):
                query3(2 * i, 0, False)
                query3(2 * i + 1, 1, False)

            tiles(1, NT // 2, 0, q_pair)

            def diag(h, par, i, first):
                dve.wait_ge(head_in[par], 32 * i + 32)
                if not first:
                    dve.wait_ge(conv_done, h - 1)
                dve.scalar_tensor_tensor(tdiag[:, par, :], ident[:, :], D_b[:, bass.ds(h, 1)], toep_s[:, par, 0, :], ALU.mult, ALU.add).then_inc(tdiag_ready, 1)

            def times_q(h, par):
                dve.wait_ge(conv_done, h + 1)
                R = prods[:, par, :].rearrange("p (g b j s) -> p g b j s", g=4, b=8, j=HD)
                Y = psum[:, 4 * par:4 * par + 4, 0:8 * NPR].rearrange("p g (b r) -> p g b r", r=NPR)
                at = 0
                for d in range(HD):
                    n = HD - d
                    y = Y[:, :, :, at:at + n]
                    q0 = qT[:, :, :, bass.ds(h * HD, n)].rearrange("p l (g b) i -> p (l g) b i", g=2)
                    m = dve.tensor_tensor(R[:, :, :, d:HD, d], y, q0, ALU.mult)
                    if d:
                        q1 = qT[:, :, :, bass.ds(h * HD + d, n)].rearrange("p l (g b) i -> p (l g) b i", g=2)
                        m = dve.tensor_tensor(R[:, :, :, 0:n, HD - d], y, q1, ALU.mult)
                    at += n
                m.then_inc(prod_done, 1)
                dve.wait_ge(prod_done, h + 1)
                dve.tensor_reduce(OT[:, :, :, bass.ds(h * HD, HD)].rearrange("p l b j -> p (l b) j"),
                                  prods[:, par, :].rearrange("p (r j s) -> p r j s", j=HD, s=HD), AX.X, ALU.add).then_inc(o3_ready, 1)

            dve.wait_ge(qT_ready, NT)
            diag(0, 0, 0, True)
            diag(1, 1, 0, True)
            times_q(0, 0)
            with dve.Fori(1, NH // 2) as i:
                diag(2 * i, 0, i, False)
                times_q(2 * i - 1, 1)
                diag(2 * i + 1, 1, i, False)
                times_q(2 * i, 0)
            times_q(NH - 1, 1)
            for b in range(NT):
                dve.wait_ge(o3T_done, b + 1)
                dve.scalar_tensor_tensor(X[:, b, :], psum[:, b % 4, 0:D], tg[:, 2:3], X[:, b, :], ALU.mult, ALU.add).then_inc(x3_done, 1)
                dve.wait_ge(x3_done, b + 1)
                moments(X[:, b, :], b)
            variance(5)
            dve.wait_ge(rstd_ready, 5)


            dve.wait_ge(c_done, 2)
            R = 22
            start = v["at"] + v["k"]
            with dve.Fori(0, NPAIR // 2) as i:
                v["at"], v["k"] = start + i * R, 0
                for par in range(2):
                    u = 2 * i + par
                    for q in range(2):
                        dve.tensor_scalar(hst[:, par, q, :], X[:, 2 * u + q, :], mv[:, 2 * u + q, 0:1], rstd[:, bass.ds(2 * u + q, 1)], ALU.subtract, ALU.mult)
                        m = dve.tensor_scalar(H[:, 2 * u + q, 0:D], X[:, 2 * u + q, :], mv[:, 2 * u + q, 0:1], rstd[:, bass.ds(2 * u + q, 1)], ALU.subtract, ALU.mult)
                    m.then_inc(h_ready, 1)
                    dve.wait_ge(logits_done, u + 1)
                    link(dve.tensor_copy(lg[:, :, :], pA[par][:, 0:2 * E].rearrange("p (q e) -> p q e", q=2)))
                    alone(dve, "dve")
                    dve.max(top8[:, 0, :], lg[:, 0, :])
                    link(dve.max(top8[:, 1, :], lg[:, 1, :]))
                    dve.tensor_scalar(negmax[:, :], top8[:, :, 0], -1.0, None, ALU.mult).then_inc(negmax_ready, 1)
                    dve.max_index(idx8[:, 0, :], top8[:, 0, :], lg[:, 0, :])
                    link(dve.max_index(idx8[:, 1, :], top8[:, 1, :], lg[:, 1, :]))
                    link(dve.tensor_copy(idxf[:, :, :], idx8[:, :, :]))
                    for q in range(2):
                        dve.tensor_copy(H[:, 2 * u + q, CE:CE + K], idxf[:, q, 0:K])
                    for q in range(2):
                        m = dve.tensor_tensor(oh[:, q], iota_e[:, None, :].to_broadcast([P, K, E]),
                                          idxf[:, q, 0:K, None].to_broadcast([P, K, E]), ALU.is_equal)
                    link(m)
                    dve.tensor_reduce(mask[:, :, :], oh[:, :, :, :].rearrange("p q k e -> p q e k"), AX.X, ALU.max).then_inc(mask_ready, 1)
                    dve.wait_ge(exp_done, u + 1)
                    link(dve.tensor_reduce(den[:, :, 0], e6[:, :, :], AX.X, ALU.add))
                    link(dve.scalar_tensor_tensor(den[:, :, 1], sum64[:, :], 1e-20, den[:, :, 0], ALU.mult, ALU.add))
                    link(dve.reciprocal(den[:, :, 0], den[:, :, 1]))
                    for q in range(2):
                        dve.tensor_scalar(H[:, 2 * u + q, CW:CW + K], e6[:, q, :], den[:, q, 0:1], tg[:, 3:4], ALU.mult, ALU.mult)
                    dve.wait_ge(rank_done, u + 1)
                    dve.tensor_tensor(msum[:, :], mask[:, 0, :], mask[:, 1, :], ALU.add)
                    link(dve.tensor_tensor(posr[:, :, :], pY[par][:, 0:2 * E].rearrange("p (q e) -> p q e", q=2),
                                           iota_row[:, None, :].to_broadcast([P, 2, E]), ALU.add))
                    dve.tensor_tensor(macc[:, 1 - par, :], macc[:, par, :], msum[:, :], ALU.add)
                    for q in range(2):
                        m = dve.tensor_tensor(prod[:, q], oh[:, q], posr[:, q, None, :].to_broadcast([P, K, E]), ALU.mult)
                    link(m)
                    link(dve.tensor_reduce(slotf[:, :, :], prod[:, :, :, :], AX.X, ALU.add))
                    for q in range(2):
                        m = dve.tensor_copy(slot[:, 2 * u + q, :], slotf[:, q, :])
                    m.then_inc(slots_ready, 1)
                assert v["k"] == R
            v["at"], v["k"] = start + (NPAIR // 2) * R, 0

            dve.wait_ge(load_done, 1)
            link(dve.tensor_copy(cnt_f[:, :], pT[0][0:E, 0:P]))
            dve.tensor_copy(ov_c[:, 0, :], pT[0][:, P:P + E])
            link(dve.tensor_scalar(nb_i[:, :], cnt_f[:, :], float(-(CAP + 1 - P)), 0.0, ALU.add, ALU.max))
            link(dve.tensor_scalar(nb_j[:, :], nb_i[:, :], 7, None, ALU.logical_shift_right))
            dve.tensor_copy(nb_b[:, :], nb_j[:, :]).then_inc(nb_ready, 1)
            dve.wait_ge(ov_done, 1)
            link(dve.tensor_copy(ov_c[:, 1, :], pT[1][:, E:2 * E]))
            link(dve.tensor_scalar(ov_w[:, 0, :], pT[1][:, 0:E], pid[:, 0:1], 0.0, ALU.is_le, ALU.add, accum_out=ov_s[:, 0:1]))
            link(dve.tensor_scalar(ov_s[:, 1:2], ov_s[:, 0:1], float(E - 1), None, ALU.min))
            link(dve.scalar_tensor_tensor(ov_w[:, 1, :], iota_e[:, :], ov_s[:, 1:2], ov_c[:, 0, :], ALU.is_equal, ALU.mult, accum_out=ov_s[:, 2:3]))
            link(dve.scalar_tensor_tensor(ov_w[:, 2, :], iota_e[:, :], ov_s[:, 1:2], ov_c[:, 1, :], ALU.is_equal, ALU.mult, accum_out=ov_s[:, 3:4]))
            dve.tensor_scalar(ov_s[:, 5:6], ov_s[:, 1:2], float(T), None, ALU.mult)
            link(dve.tensor_scalar(ov_s[:, 4:5], ov_s[:, 3:4], pid[:, 0:1], -float(P), ALU.subtract, ALU.mult))
            link(dve.tensor_scalar(ov_s[:, 6:7], ov_s[:, 4:5], ov_s[:, 5:6], float(CAP), ALU.add, ALU.add))
            link(dve.tensor_scalar(ov_s[:, 8:9], ov_s[:, 2:3], -1.0, 0.0, ALU.add, ALU.max))
            link(dve.tensor_tensor(ov_s[:, 7:8], ov_s[:, 8:9], ov_s[:, 5:6], ALU.add))
            for r, c in enumerate((6, 7, 1)):
                m = dve.tensor_scalar(bvals[:, r, :], ident[:, :], 0.0, ov_s[:, c:c + 1], ALU.mult, ALU.add)
            m.then_inc(bval_ready, 1)
            dve.wait_ge(brow_done, 1)
            link(dve.tensor_copy(rows_f[:, :, :], pY[0][:, 0:3 * P].rearrange("p (v b) -> p v b", v=3)))
            link(dve.tensor_scalar(rows_f[:, 0, :], rows_f[:, 0, :], pid[:, 0:1], None, ALU.add))
            dve.tensor_tensor(gvalid[:, :], rows_f[:, 0, :], rows_f[:, 1, :], ALU.is_le)
            link(dve.tensor_scalar(gpad[:, :], rows_f[:, 0, :], dump[:, 0:1], -1.0, ALU.subtract, ALU.mult))
            link(dve.tensor_tensor(gpad[:, :], gpad[:, :], gvalid[:, :], ALU.mult))
            link(dve.tensor_tensor(gidx[:, :], gpad[:, :], rows_f[:, 0, :], ALU.add))
            dve.tensor_copy(eb_i[:, 0, :], rows_f[0:1, 2, :])
            dve.tensor_copy(eb_i[:, 1, :], rows_f[0:1, 0, :])
            dve.tensor_scalar(nov_i[:, :], pT[1][:, E - 1:E], 1.0, None, ALU.max).then_inc(ov_ready, 1)
            dve.wait_ge(ov_ready, 1)
            n = dve.value_load(nov_i[0:1, 0:1], min_val=1, max_val=MAXB)

            def shared_hidden(u, par, first):
                if not first:
                    dve.wait_ge(sy_done, u - 1)
                for c, (f0, fw) in enumerate(FS):
                    dve.wait_ge(ssilu_done, 3 * u + c + 1)
                    dve.tensor_tensor(shid[0:fw, par, c], ssil[0:fw, par, c], s_banks[par][c][0:fw, CAP:2 * CAP], ALU.mult).then_inc(shid_ready, 1)

            def shared_out(u, par):
                dve.wait_ge(sy_done, u + 1)
                for j in range(2):
                    m = dve.scalar_tensor_tensor(X[:, 2 * u + j, :], pY[par][:, j * D:(j + 1) * D], tg[:, 3:4], X[:, 2 * u + j, :], ALU.mult, ALU.add)
                m.then_inc(base_ready, 1)

            shared_hidden(0, 0, True)
            shared_hidden(1, 1, True)
            shared_out(0, 0)
            with dve.Fori(1, NPAIR // 2) as i:
                shared_hidden(2 * i, 0, False)
                shared_out(2 * i - 1, 1)
                shared_hidden(2 * i + 1, 1, False)
                shared_out(2 * i, 0)
            shared_out(NPAIR - 1, 1)

            with dve.Fori(0, n) as b:
                dve.tensor_copy(gcol[:, :], gidx[:, bass.ds(b, 1)]).then_inc(gcol_ready, 1)
                dve.wait_ge(padded, 16 * b + 16)
                alone(dve, "dve")

            def weights(i, s, first):
                e, par, turn = 4 * i + s, s % 2, 2 * i + s // 2
                dve.wait_ge(xs_in[s], 16 * i + 16)
                if not first:
                    dve.wait_ge(added[par][0], 16 * turn - 16)
                    dve.wait_ge(added[par][1], 16 * turn - 16)
                for j in range(2):
                    dve.scalar_tensor_tensor(wsel[:, s, j, :], xs_sb[:, s, j, CE:CE + K], iota_e[:, bass.ds(e, 1)],
                                             xs_sb[:, s, j, CW:CW + K], ALU.is_equal, ALU.mult, accum_out=wtok[:, s, j:j + 1])
                dve.tensor_copy(toki[:, s, :], xs_sb[:, s, :, CT]).then_inc(tok_ready, 1)

            def expert_hidden(e, par, first):
                if not first:
                    dve.wait_ge(y_done, e - 1)
                dve.wait_ge(silA_done, e + 1)
                dve.tensor_tensor(hid0[:, par], sil0[:, par], pA[par][:, CAP:2 * CAP], ALU.mult)
                dve.wait_ge(silC_done, e + 1)
                dve.tensor_tensor(hid1[:, par], sil1[:, par], pC[par][64:64 + F1, 0:CAP], ALU.mult).then_inc(xhid_ready, 1)

            def weigh(e, s):
                par = s % 2
                dve.wait_ge(tok_ready, e + 1)
                dve.wait_ge(y_done, e + 1)
                for j in range(2):
                    m = dve.tensor_scalar(y_sb[:, s, j, :], pY[par][:, j * D:(j + 1) * D], wtok[:, s, j:j + 1], None, ALU.mult)
                m.then_inc(y_ready, 1)

            weights(0, 0, True)
            weights(0, 1, True)
            expert_hidden(0, 0, True)
            weights(0, 2, True)
            expert_hidden(1, 1, True)
            weigh(0, 0)
            weights(0, 3, True)
            expert_hidden(2, 0, False)
            weigh(1, 1)
            with dve.Fori(1, E // 4) as i:
                for s in range(4):
                    weights(i, s, False)
                    expert_hidden(4 * i + s - 1, (s - 1) % 2, False)
                    weigh(4 * i + s - 2, (s - 2) % 4)
            expert_hidden(E - 1, 1, False)
            weigh(E - 2, 2)
            weigh(E - 1, 3)

            dve.wait_ge(added[0][0], 16 * (E // 2))
            dve.memset(ovcol[:, 1:2], 0.0).then_inc(o_yr, 1)
            with dve.Fori(0, n) as b:
                dve.tensor_copy(ovcol[:, 0:1], rows_f[:, 2, bass.ds(b, 1)]).then_inc(o_col, 1)
                dve.wait_ge(o_x, 16 * b + 16)
                dve.wait_ge(o_col, b + 1)
                alone(dve, "dve")
                dve.scalar_tensor_tensor(wsel[:, 0, 0, :], xs_sb[:, 0, 0, CE:CE + K], ovcol[:, 0:1],
                                         xs_sb[:, 0, 0, CW:CW + K], ALU.is_equal, ALU.mult, accum_out=wtok[:, 0, 0:1])
                dve.tensor_copy(toki[:, 0, 0:1], xs_sb[:, 0, 0, CT:CT + 1]).then_inc(o_tok, 1)
                dve.wait_ge(o_silu, b + 1)
                dve.tensor_tensor(hid0[:, 0, 0:P], sil0[:, 0, 0:P], pA[0][:, P:2 * P], ALU.mult)
                dve.tensor_tensor(hid1[:, 0, 0:P], sil1[:, 0, 0:P], pC[0][64:64 + F1, 0:P], ALU.mult).then_inc(o_hid, 1)
                dve.wait_ge(o_tok, b + 1)
                dve.wait_ge(o_y, b + 1)
                dve.tensor_scalar(y_sb[:, 0, 0, :], pY[0][:, 0:D], wtok[:, 0, 0:1], None, ALU.mult).then_inc(o_yr, 1)
                dve.wait_ge(o_add, 16 * b + 16)
                alone(dve, "dve")

            for c in range(4):
                dve.wait_ge(back_in[c], 64)
                xc = X[:, 4 * c:4 * c + 4, :]
                for q in range(4):
                    m = dve.tensor_tensor(xc, xc, back[:, q, 4 * c:4 * c + 4, :], ALU.add)
                    if q < 3:
                        link(m)
                m.then_inc(sum_done, 1)



def kernel(**inputs):
    import numpy as np
    import concourse.bacc as bacc
    from concourse.bass_utils import run_bass_kernel_spmd

    def toeplitz(k):
        p = np.concatenate([np.zeros((16, 128), k.dtype), k], 1)
        i = np.arange(128)[None, None, :] - np.arange(128)[None, :, None]
        return np.stack([p[:, 128 + i[0]], p[:, 256 + i[0]]], 2).reshape(16, 128, 256)

    def expert_weights(w, down):
        w = w.reshape(64, 352, 2, 128).transpose(0, 3, 2, 1)
        o = np.zeros((64, 128, 2, 368), w.dtype)
        o[..., 0:128] = w[..., 0:128]
        o[..., 128:256] = w[..., 176:304]
        o[..., 256:304] = w[..., 128:176]
        o[..., 320:368] = w[..., 304:352]
        return np.concatenate([o.reshape(64, 128, 736), down[:, 0:128]], 2)

    a = {k: np.asarray(v) for k, v in inputs.items()}
    c = a["ctx_2048"]
    down = a["L1_ffn_w_down"].transpose(0, 2, 1)
    arrays = {
        "x": a["x"],
        "ctxn": c,
        "ctxT": c.transpose(0, 2, 1),
        "ctxH": c.reshape(16, 16, 8, 2, 128).transpose(1, 4, 3, 0, 2).reshape(16, 128, 256 * 2 // 2),
        "toep": toeplitz(a["L1_xattn_ssm_kernel"]),
        "gates": np.stack([a["g_xattn"], a["g_ffn"]], 1).reshape(4),
        "wsynT": a["L0_ffn_W_syn"].T,
        "woutT": a["L0_ffn_W_out"].T,
        "bsyn": a["L0_ffn_b_syn"],
        "bout": a["L0_ffn_b_out"],
        "gamma": a["L0_ffn_gamma"],
        "beta": a["L0_ffn_beta"],
        "ssm_D": a["L1_xattn_D"],
        "gateT": a["L1_ffn_gate_w"].reshape(64, 2, 128).transpose(2, 1, 0),
        "wexp": expert_weights(a["L1_ffn_w_gate_up"], down),
        "wd1": down[:, 128:],
        "wsgu": a["L1_ffn_ws_gate_up"].reshape(704, 2, 128).transpose(2, 1, 0),
        "wsd": a["L1_ffn_ws_down"].T,
    }
    arrays = {"in_" + k: np.ascontiguousarray(v) for k, v in arrays.items()}
    nc = bacc.Bacc("TRN2", target_bir_lowering=False, num_devices=1)
    args = [nc.dram_tensor(n, v.shape, mybir.dt.from_np(v.dtype), kind="ExternalInput").ap() for n, v in arrays.items()]
    args.append(nc.dram_tensor("out_0", (16, 128, 256), mybir.dt.float32, kind="ExternalOutput").ap())
    build(nc, *args)
    r = run_bass_kernel_spmd(nc, [arrays], core_ids=[0])
    return r.results[0]["out_0"]
```

```python
import concourse.bass as bass
from concourse import mybir
from contextlib import ExitStack


def build(nc, x, ctxn, ctxT, ctxH, toep, gates_in, wsynT, woutT, bsyn, bout, gamma, beta, ssm_D,
          gateT, wexp, wd1, wsgu, wsd, out):
    f32, bf16, i32, u32 = mybir.dt.float32, mybir.dt.bfloat16, mybir.dt.int32, mybir.dt.uint32
    ALU = mybir.AluOpType
    ACT = mybir.ActivationFunctionType
    AX = mybir.AxisListType

    P = 128
    NT = 16
    D = 256
    N = 1024
    NH, HD = 16, 8
    NPR = HD * (HD + 1) // 2
    OS = 320
    TOPK = 102
    ROUNDS = 5
    AIM, NEAR = TOPK - 4, TOPK - 8
    FAR = 60.0
    BIG = 2.0 ** 64
    SIG = 13.3
    DENS = N * 0.1755
    NTD = 8

    T = NT * P
    E = 64
    K = 6
    F = 176
    F1 = F - P
    GU = 368
    CAP = 256
    ROW = 272
    CT, CE, CW = D, D + 1, D + 1 + K
    FS = [(0, P), (P, P), (2 * P, 96)]
    FSH = 352
    MAXB = 96
    NPAIR = NT // 2

    xs_rows = nc.dram_tensor("xs_rows", (E * T + P, ROW), f32, kind="Internal").ap()
    rows_v = xs_rows[0:E * T, :].rearrange("(e c) d -> e c d", c=T)
    acc = [nc.dram_tensor(f"acc{i}", (T + P, D), f32, kind="Internal").ap() for i in range(4)]

    with ExitStack() as ctx:
        def sb(name, shape, dt=f32):
            return ctx.enter_context(nc.sbuf_tensor(name, shape, dt))

        def sem(name):
            return ctx.enter_context(nc.semaphore(name))

        X = sb("X", [P, NT, D])
        Z = sb("Z", [P, NT * N])
        z = Z[:, :].rearrange("p (t n) -> p t n", n=N)
        wraw = Z[:, 0:4 * N].rearrange("p (a n) -> p a n", a=4)
        prods = Z[:, 8448:8448 + 4096].rearrange("p (a n) -> p a n", a=2)
        kv = Z[:, 12544:12544 + 4 * NT * NPR].rearrange("p (a m b r) -> p a m b r", a=2, m=2, b=NT)
        H2 = sb("H2", [P, NT, D])
        OT = H2[:, :, :].rearrange("p b (c d) -> p (b c) d", c=2).rearrange("p (l b) d -> p l b d", l=2)
        qT = sb("qT", [P, 2, NT, P])
        wt = sb("wt", [P, 4, N])
        wsyn = wt[:, 0:2, :]
        wout = wt[:, 2:4, :].rearrange("p a n -> p (a n)").rearrange("p (c d) -> p c d", c=8)
        hh = sb("hh", [P, 4, N])
        hidden, hidT = hh[:, 0:2, :], hh[:, 2:4, :]
        attn = hidT[:, 0, :].rearrange("p (a e d) -> p a e d", a=2, e=2)
        qn = hidT[:, 1, 0:512].rearrange("p (a d) -> p a d", a=2)
        vTs = hidT[:, 1, 512:1024].rearrange("p (a e s) -> p a e s", a=2, e=2)
        ctx_s = sb("ctx_s", [P, 2, D])
        ctxT_s = sb("ctxT_s", [P, 2, 2, P])
        ctxH_s = sb("ctxH_s", [P, 2, 2, NT, HD])
        toep_s = sb("toep_s", [P, 2, 2, P])
        tdiag = sb("tdiag", [P, 2, P])
        hs = sb("hs", [P, 2, D])
        hTs = sb("hTs", [P, 2, 2, P])
        bsyn_b = sb("bsyn_b", [P, N])
        bout_b = sb("bout_b", [P, D])
        gam_b = sb("gam_b", [P, D])
        bet_b = sb("bet_b", [P, D])
        D_b = sb("D_b", [P, NH])
        ident = sb("ident", [P, P])
        onesf = sb("onesf", [P, P])
        neghalf = sb("neghalf", [P, NT])
        iota9 = sb("iota9", [P, 9])
        gates = sb("gates", [P, 4])
        tg = sb("tg", [P, 4])
        stats = sb("stats", [P, NT, 6])
        eps2 = sb("eps2", [P, 2])
        mv = sb("mv", [P, NT, 2])
        mvt = sb("mvt", [P, NT, 2])
        rstd = sb("rstd", [P, NT])
        smax = sb("smax", [P, 2])
        nsmax = sb("nsmax", [P, 2, 2])
        asum = sb("asum", [P, 2, 2])
        rsum = sb("rsum", [P, 2])
        wabs = sb("wabs", [P, 2])
        wsc = sb("wsc", [P, 2])
        wcut = sb("wcut", [P, 2])
        wneg = sb("wneg", [P, 2])
        spread = sb("spread", [P, 2])
        thr = sb("thr", [P, NT])
        nthr = sb("nthr", [P, NT])
        cnt = sb("cnt", [P, NT])
        lo = sb("lo", [P, NT]); clo = sb("clo", [P, NT])
        hi = sb("hi", [P, NT]); chi = sb("chi", [P, NT])
        up = sb("up", [P, NT], u32); dn = sb("dn", [P, NT], u32)
        t1 = sb("t1", [P, NT]); t2 = sb("t2", [P, NT]); t3 = sb("t3", [P, NT])
        m8 = sb("m8", [P, 2, 8])
        hib = sb("hib", [P, NT]); below = sb("below", [P, NT])
        m9 = sb("m9", [P, NT, 9])
        m9s = sb("m9s", [P, NT, 9])
        bad = sb("bad", [P, 1])
        bad_i = sb("bad_i", [P, 1], i32)

        H = Z[:, 0:NT * ROW].rearrange("p (t d) -> p t d", t=NT)
        back = [b.rearrange("p (t d) -> p t d", t=NT) for b in (qT[:, :, :, :].rearrange("p l b i -> p (l b i)"), Z[:, 0:NT * D],
                                                                Z[:, NT * D:2 * NT * D], Z[:, 11616:11616 + NT * D])]
        H2f = H2[:, :, :].rearrange("p t d -> p (t d)")
        shid = H2f[:, 0:1536].rearrange("p (a c t) -> p a c t", a=2, c=3)
        ssil = H2f[:, 1536:3072].rearrange("p (a c t) -> p a c t", a=2, c=3)
        sil0 = H2f[:, 3072:3584].rearrange("p (a t) -> p a t", a=2)
        sil1 = H2f[0:F1, 3584:4096].rearrange("p (a t) -> p a t", a=2)
        qTf = qT[:, :, :, :].rearrange("p l b i -> p (l b i)")
        hid0 = qTf[:, 0:512].rearrange("p (a t) -> p a t", a=2)
        hid1 = qTf[0:F1, 512:1024].rearrange("p (a t) -> p a t", a=2)
        xs_sb = Z[:, 8448:8448 + 8 * ROW].rearrange("p (a b d) -> p a b d", a=4, b=2)
        w_sb = Z[:, 10624:10624 + 4 * (2 * GU + D)].rearrange("p (a f) -> p a f", a=4)
        xT = qTf[:, 2176:2176 + 1024].rearrange("p (a k t) -> p a k t", a=2, k=2)
        wtf = wt[:, :, :].rearrange("p a n -> p (a n)")
        wsgu_sb = wtf[:, 0:2 * 2 * FSH].rearrange("p (k f) -> p k f", k=2)
        wgu_sb = w_sb[:, :, 0:2 * GU].rearrange("p a (k f) -> p a k f", k=2)
        wd0_sb = w_sb[:, :, 2 * GU:2 * GU + D]
        wd1_sb = wtf[0:F1, 1408:1408 + 4 * D].rearrange("p (a d) -> p a d", a=4)
        hidf = hidden[:, :, :].rearrange("p a n -> p (a n)")
        oh = hidf[:, 0:4 * K * E].rearrange("p (a q k e) -> p a q k e", a=2, q=2, k=K)
        hidTf = hidT[:, :, :].rearrange("p a n -> p (a n)")
        prod = hidTf[:, 0:2 * K * E].rearrange("p (q k e) -> p q k e", q=2, k=K)
        y_sb = hidTf.rearrange("p (a b d) -> p a b d", a=4, b=2)
        hst = hidTf[:, 1024:1024 + 4 * D].rearrange("p (a q d) -> p a q d", a=2, q=2)
        fill = sb("fill", [P, 2, ROW])
        wsd_sb = sb("wsd_sb", [P, 3, D])
        gate_sb = sb("gate_sb", [P, 2, E])
        tri = sb("tri", [P, P], bf16)
        trii = sb("trii", [E, E], bf16)
        ones = sb("ones", [P, P], bf16)
        iota_e = sb("iota_e", [P, E])
        iota_row = sb("iota_row", [P, E])
        pid = sb("pid", [P, 1])
        dump = sb("dump", [P, 1])
        lg = sb("lg", [P, 2, 2, E])
        top8 = sb("top8", [P, 2, 2, 8])
        idx8 = sb("idx8", [P, 2, 2, 8], u32)
        idxf = sb("idxf", [P, 2, 2, 8])
        negmax = sb("negmax", [P, 2, 2])
        e64 = sb("e64", [P, 2, 2, E])
        sum64 = sb("sum64", [P, 2, 2])
        e6 = sb("e6", [P, 2, 2, K])
        den = sb("den", [P, 2, 2])
        mask = sb("mask", [P, 2, 2, E], bf16)
        macc = sb("macc", [P, 2, E], bf16)
        msum = sb("msum", [P, E], bf16)
        posr = sb("posr", [P, 2, E])
        slotf = sb("slotf", [P, 2, K])
        slot = sb("slot", [P, NT, K], i32)
        wsel = sb("wsel", [P, 4, 2, K])
        wtok = sb("wtok", [P, 4, 2])
        toki = sb("toki", [P, 4, 2], i32)
        cnt_f = sb("cnt_f", [E, P])
        nb_i = sb("nb_i", [E, P], i32)
        nb_j = sb("nb_j", [E, P], i32)
        nb_b = sb("nb_b", [E, P], bf16)
        ov_s = sb("ov_s", [P, 12])
        ov_w = sb("ov_w", [P, 3, E])
        ov_c = sb("ov_c", [P, 2, E])
        bvals = sb("bvals", [P, 3, P])
        rows_f = sb("rows_f", [P, 3, P])
        gidx = sb("gidx", [P, P], i32)
        gvalid = sb("gvalid", [P, P])
        gpad = sb("gpad", [P, P])
        eb_i = sb("eb_i", [1, 2, P], i32)
        nov_i = sb("nov_i", [P, 1], i32)
        gcol = sb("gcol", [P, 1], i32)
        ovcol = sb("ovcol", [P, 2])
        psum = ctx.enter_context(nc.psum_tensor("psum", [P, 8, 512], f32))
        banks = [psum[:, i, :] for i in range(8)]
        pT, pA, pC, pY = banks[0:2], banks[2:4], banks[4:6], banks[6:8]
        r_turn, r_log = banks[0], [banks[1], banks[7]]
        s_up, s_y = banks[2:5], banks[5:7]
        junk = qT[:, :, :, :].rearrange("p l b i -> p (l b i)").bitcast(bf16).rearrange("p (t n) -> p t n", n=N)
        ajunk = hh[:, :, :].rearrange("p a n -> p (a n)").bitcast(bf16).rearrange("p (t n) -> p t n", n=N)

        x_in = [sem(f"x_in{c}") for c in range(4)]
        small_in = sem("small_in")
        wraw_in = sem("wraw_in")
        consts = sem("consts")
        w_ready = sem("w_ready")
        wabs_ready = sem("wabs_ready")
        wsum_done = sem("wsum_done")
        tg_ready = sem("tg_ready")
        var_ready = sem("var_ready")
        rstd_ready = sem("rstd_ready")
        var2_ready, rstd2_ready = sem("var2_ready"), sem("rstd2_ready")
        var3_ready, rstd3_ready = sem("var3_ready"), sem("rstd3_ready")
        var4_ready, rstd4_ready = sem("var4_ready"), sem("rstd4_ready")
        stats_done, var5_ready, rstd5_ready = sem("stats_done"), sem("var5_ready"), sem("rstd5_ready")
        qn_ready = sem("qn_ready")
        sc_done = sem("sc_done")
        smax_ready = sem("smax_ready")
        attn_ready = sem("attn_ready")
        v_scaled = sem("v_scaled")
        pv_done = sem("pv_done")
        x1_done = sem("x1_done")
        hs_ready = sem("hs_ready")
        hT_full = sem("hT_full")
        hT_ready = sem("hT_ready")
        z_done = sem("z_done")
        z_ready = sem("z_ready")
        h2b_done = sem("h2b_done")
        thr_ready = sem("thr_ready")
        cnt_done = sem("cnt_done")
        masked = sem("masked")
        max_done = sem("max_done")
        above_done = sem("above_done")
        below_done = sem("below_done")
        bad_ready = sem("bad_ready")
        bad_done = sem("bad_done")
        hid_ready = sem("hid_ready")
        hidT_full = sem("hidT_full")
        hidT_ready = sem("hidT_ready")
        o_done = sem("o_done")
        qs_ready = sem("qs_ready")
        qT_full = sem("qT_full")
        qT_ready = sem("qT_ready")
        tdiag_ready = sem("tdiag_ready")
        kv_ready = sem("kv_ready")
        conv_done = sem("conv_done")
        prod_done = sem("prod_done")
        halves_ready = sem("halves_ready")
        osum_done = sem("osum_done")
        o3_ready = sem("o3_ready")
        o3T_done = sem("o3T_done")
        x3_done = sem("x3_done")
        out_done = sem("out_done")
        v_step = sem("v_step")
        p_step = sem("p_step")
        l_step = sem("l_step")
        gate_in = sem("gate_in")
        ws_in = sem("ws_in")
        xhid_ready = sem("xhid_ready")
        load_done = sem("load_done")
        c_done = sem("c_done")
        filled = sem("filled")
        h_ready = sem("h_ready")
        rT_full = sem("rT_full")
        rT_ready = sem("rT_ready")
        logits_done = sem("logits_done")
        negmax_ready = sem("negmax_ready")
        exp_done = sem("exp_done")
        mask_ready = sem("mask_ready")
        rank_done = sem("rank_done")
        slots_ready = sem("slots_ready")
        scattered = sem("scattered")
        sgu_done = sem("sgu_done")
        ssilu_done = sem("ssilu_done")
        shid_ready = sem("shid_ready")
        sy_done = sem("sy_done")
        base_ready = sem("base_ready")
        xT_full = sem("xT_full")
        xT_ready = sem("xT_ready")
        guA_done = sem("guA_done")
        guC_done = sem("guC_done")
        silA_done = sem("silA_done")
        silC_done = sem("silC_done")
        y_done = sem("y_done")
        y_ready = sem("y_ready")
        tok_ready = sem("tok_ready")
        nb_ready = sem("nb_ready")
        ov_done = sem("ov_done")
        bval_ready = sem("bval_ready")
        brow_done = sem("brow_done")
        ov_ready = sem("ov_ready")
        padded = sem("padded")
        gcol_ready = sem("gcol_ready")
        o_w = sem("o_w")
        o_col = sem("o_col")
        o_tok = sem("o_tok")
        o_x = sem("o_x")
        o_T = sem("o_T")
        o_Tr = sem("o_Tr")
        o_gu = sem("o_gu")
        o_silu = sem("o_silu")
        o_hid = sem("o_hid")
        o_y = sem("o_y")
        o_yr = sem("o_yr")
        o_add = sem("o_add")
        zeroed = sem("zeroed")
        sum_done = sem("sum_done")
        sum3_step, early_in = sem("sum3_step"), sem("early_in")
        back_in = [sem(f"back_in{c}") for c in range(4)]
        added = [[sem(f"added{q}{j}") for j in range(2)] for q in range(2)]
        w_in = [sem(f"w_in{s}") for s in range(4)]
        xs_in = [sem(f"xs_in{s}") for s in range(4)]
        ctx_in = [sem("ctx_in0"), sem("ctx_in1")]
        head_in = [sem("head_in0"), sem("head_in1")]
        tick = {n: sem("tick_" + n) for n in ("pool", "dve", "sp", "pe", "act")}

        def alone(eng, name):
            eng.sem_inc(tick[name], 1)


        def there(t):
            return type(t) is not int or 0 <= t < NT

        def later(t):
            return type(t) is not int or t >= 2

        EARLY, LATE = 6, NT - 2

        def pipeline(eng, first, last, body):
            for b in range(first, EARLY):
                body(b, b % 2)
            with eng.Fori(EARLY // 2, LATE // 2) as i:
                body(2 * i, 0)
                body(2 * i + 1, 1)
            for b in range(LATE, last + 1):
                body(b, b % 2)

        block = ctx.enter_context(nc.Block())

        def bc(ap, n):
            return ap.rearrange("(a n) -> a n", a=1).to_broadcast([P, n])

        @block.sync
        def _(sp):
            def load_x(c):
                sp.dma_start(X[:, 4 * c:4 * c + 4, :], x[4 * c:4 * c + 4].rearrange("b p d -> p b d")).then_inc(x_in[c], 16)

            def load_ctx(b, par):
                sp.dma_start(ctx_s[:, par, :], ctxn[b]).then_inc(ctx_in[par], 16)
                sp.dma_start(ctxT_s[:, par], ctxT[b].rearrange("(k p) s -> p k s", p=P)).then_inc(ctx_in[par], 16)

            load_x(0)
            load_ctx(0, 0)
            load_ctx(1, 1)
            for c in range(1, 4):
                load_x(c)
            sp.dma_start(wraw[:, 0:2, :], wsynT.rearrange("(k p) n -> p k n", p=P)).then_inc(wraw_in, 16)
            sp.dma_start(wraw[:, 2:4, :].rearrange("p a n -> p (a n)").rearrange("p (c d) -> p c d", c=8),
                         woutT.rearrange("(c p) d -> p c d", p=P)).then_inc(wraw_in, 16)
            with sp.Fori(1, NT // 2) as i:
                for par in range(2):
                    b = 2 * i + par
                    sp.wait_ge(sc_done, b - 1)
                    sp.wait_ge(v_scaled, b - 1)
                    alone(sp, "sp")
                    load_ctx(b, par)

            def load_head(h, par):
                sp.dma_start(ctxH_s[:, par].rearrange("p l b i -> p (l b i)"), ctxH[h]).then_inc(head_in[par], 16)
                sp.dma_start(toep_s[:, par].rearrange("p c l -> p (c l)"), toep[h]).then_inc(head_in[par], 16)

            load_head(0, 0)
            load_head(1, 1)
            with sp.Fori(1, NH // 2) as i:
                for par in range(2):
                    h = 2 * i + par
                    sp.wait_ge(kv_ready, h - 1)
                    sp.wait_ge(conv_done, h - 1)
                    alone(sp, "sp")
                    load_head(h, par)

            sp.dma_start(gate_sb[:, :, :], gateT).then_inc(gate_in, 16)
            sp.dma_start(wsd_sb[:, 0:2, :], wsd[0:2 * P, :].rearrange("(c p) d -> p c d", p=P)).then_inc(ws_in, 16)
            sp.dma_start(wsd_sb[0:96, 2, :], wsd[2 * P:FSH, :]).then_inc(ws_in, 16)
            sp.wait_ge(o_done, NT)
            sp.dma_start(wsgu_sb, wsgu).then_inc(ws_in, 16)

            def load_weights(e, s, done):
                sp.dma_start(w_sb[:, s, :], wexp[e]).then_inc(done, 16)
                sp.dma_start(wd1_sb[:, s, :], wd1[e]).then_inc(done, 16)

            def load_rows(e, s):
                sp.dma_start(xs_sb[:, s].rearrange("p b d -> p (b d)"),
                             rows_v[e, 0:CAP, :].rearrange("(p b) d -> p (b d)", b=2)).then_inc(xs_in[s], 16)

            sp.wait_ge(o3_ready, 2 * NH)
            for s in range(4):
                load_weights(s, s, w_in[s])
            sp.wait_ge(scattered, 16 * NT * K)
            for s in range(4):
                load_rows(s, s)
            with sp.Fori(1, E // 4) as i:
                for s in range(4):
                    e = 4 * i + s
                    sp.wait_ge(tok_ready, e - 3)
                    sp.wait_ge(y_done, e - 3)
                    load_rows(e, s)
                    load_weights(e, s, w_in[s])
            sp.wait_ge(ov_ready, 1)
            sp.wait_ge(tok_ready, E - 3)
            sp.wait_ge(y_done, E - 3)
            n = sp.value_load(nov_i[0:1, 0:1], min_val=1, max_val=MAXB)
            with sp.Fori(0, n) as b:
                e = sp.value_load(eb_i[0:1, 0, bass.ds(b, 1)], min_val=0, max_val=E - 1)
                row = sp.value_load(eb_i[0:1, 1, bass.ds(b, 1)], min_val=0, max_val=E * T - P)
                sp.wait_ge(o_yr, b + 1)
                alone(sp, "sp")
                sp.dma_start(xs_sb[:, 0, 0, :], xs_rows[bass.ds(row, P), :]).then_inc(o_x, 16)
                load_weights(e, 0, o_w)
            sp.wait_ge(o_yr, n + 1)
            alone(sp, "sp")
            sp.wait_ge(o_add, 16 * n)
            alone(sp, "sp")
            for c in range(4):
                sp.dma_start(back[0][:, 4 * c:4 * c + 4, :],
                             acc[0][c * 4 * P:(c + 1) * 4 * P, :].rearrange("(t p) d -> p t d", p=P)).then_inc(back_in[c], 16)
            for c in range(4):
                if c < 3:
                    sp.wait_ge(sum_done, c + 1)
                else:
                    sp.wait_ge(sum3_step, 4)
                sp.dma_start(out[4 * c:4 * c + 4].rearrange("t p d -> p t d"), X[:, 4 * c:4 * c + 4, :]).then_inc(out_done, 16)
            sp.wait_ge(out_done, 64)

        @block.gpsimd
        def _(pool):
            pool.memset(ident[:, :], 0.0)
            pool.memset(onesf[:, :], 1.0)
            pool.memset(eps2[:, 0:1], 0.0)
            pool.memset(eps2[:, 1:2], 1e-5)
            pool.memset(neghalf[:, :], -0.5).then_inc(p_step, 1)
            pool.wait_ge(p_step, 1)
            pool.affine_select(out=ident[:, :], in_=ident[:, :], compare_op=ALU.not_equal, fill=1.0,
                               base=0, pattern=[[-1, P]], channel_multiplier=1)
            pool.iota(iota9[:, :], pattern=[[1, 9]], base=0, channel_multiplier=0,
                      allow_small_or_imprecise_dtypes=True).then_inc(consts, 1)

            def pow_input(c):
                pool.wait_ge(var_ready, c + 1)
                pool.tensor_tensor(rstd[:, 4 * c:4 * c + 4], mv[:, 4 * c:4 * c + 4, 1], neghalf[:, 0:4], ALU.pow).then_inc(rstd_ready, 1)

            pool.memset(tri[:, :], 1.0)
            pool.memset(trii[:, :], 1.0)
            pool.memset(ones[:, :], 1.0)
            pool.memset(macc[:, 0, :], 0.0)
            pool.memset(fill[:, :, :], 0.0).then_inc(p_step, 1)
            pool.wait_ge(p_step, 2)
            pool.affine_select(out=tri[:, :], in_=tri[:, :], compare_op=ALU.is_gt, fill=0.0,
                               base=0, pattern=[[1, P]], channel_multiplier=-1)
            pool.affine_select(out=trii[:, :], in_=trii[:, :], compare_op=ALU.is_ge, fill=0.0,
                               base=0, pattern=[[1, E]], channel_multiplier=-1)
            for t_, base, pat, cm in ((iota_e, 0, [[1, E]], 0), (iota_row, 0, [[T, E]], 0), (pid, 0, [[0, 1]], 1),
                                      (dump, E * T, [[0, 1]], 1)):
                pool.iota(t_[:, :], pattern=pat, base=base, channel_multiplier=cm, allow_small_or_imprecise_dtypes=True)
            pow_input(0)

            def pow_tile(t, ready, done):
                pool.wait_ge(ready, t + 1)
                alone(pool, "pool")
                pool.tensor_tensor(rstd[:, bass.ds(t, 1)], mv[:, t, 1:2], neghalf[:, 0:1], ALU.pow).then_inc(done, 1)

            def first_blocks(b, par):
                if type(b) is int and b < 4:
                    pow_input(b)
                if there(b - 1):
                    pow_tile(b - 1, var2_ready, rstd2_ready)
                if there(b - 2):
                    pool.wait_ge(hs_ready, b - 1)
                    pool.tensor_tensor(H2[:, b - 2, :], hs[:, par, :], bout_b[:, :], ALU.add)
                    pool.tensor_tensor(X[:, b - 2, :], X[:, b - 2, :], bet_b[:, :], ALU.add).then_inc(h2b_done, 1)

            pipeline(pool, 1, NT + 1, first_blocks)

            for a_ in acc:
                for c in range(T // P // 8):
                    pool.dma_start(a_[8 * c * P:8 * (c + 1) * P, :].rearrange("(p r) d -> p r d", r=8),
                                   fill[:, 0:1, 0:D].to_broadcast([P, 8, D])).then_inc(zeroed, 16)
                pool.dma_start(a_[T:T + P, :], fill[:, 0, 0:D]).then_inc(zeroed, 16)
            pool.wait_ge(zeroed, 16 * 12)
            pool.iota(fill[:, :, CT:CT + 1], pattern=[[0, 2], [0, 1]], base=T, channel_multiplier=1,
                      allow_small_or_imprecise_dtypes=True).then_inc(c_done, 1)
            pool.wait_ge(c_done, 1)
            with pool.Fori(0, E) as i:
                pool.dma_start(rows_v[i, 0:CAP, :].rearrange("(p b) d -> p (b d)", b=2),
                               fill[:, :, :].rearrange("p b d -> p (b d)")).then_inc(filled, 16)

            def norms(b, par):
                if there(b):
                    pow_tile(b, var3_ready, rstd3_ready)
                if there(b - 1):
                    pow_tile(b - 1, var4_ready, rstd4_ready)

            pipeline(pool, 0, NT, norms)

            def products(h, par, i, first):
                pool.wait_ge(head_in[par], 32 * i + 32)
                if not first:
                    pool.wait_ge(conv_done, h - 1)
                at = 0
                for d in range(HD):
                    m = pool.tensor_tensor(kv[:, par, :, :, at:at + HD - d], ctxH_s[:, par, :, :, 0:HD - d],
                                           ctxH_s[:, par, :, :, d:HD], ALU.mult)
                    at += HD - d
                m.then_inc(kv_ready, 1)

            pool.wait_ge(hid_ready, NT)
            products(0, 0, 0, True)
            products(1, 1, 0, True)
            with pool.Fori(1, NH // 2) as i:
                products(2 * i, 0, i, False)
                products(2 * i + 1, 1, i, False)

            pool.iota(H[:, :, CT:CT + 1], pattern=[[P, NT], [0, 1]], base=0, channel_multiplier=1, allow_small_or_imprecise_dtypes=True)
            pool.memset(H[:, :, CW + K:ROW], 0.0).then_inc(c_done, 1)
            for g in range(4):
                pool.wait_ge(var5_ready, g + 1)
                pool.tensor_tensor(rstd[:, 4 * g:4 * g + 4], mv[:, 4 * g:4 * g + 4, 1], neghalf[:, 0:4], ALU.pow).then_inc(rstd5_ready, 1)
            pool.wait_ge(filled, 16 * E)
            for i in range(NPAIR // 2):
                for par in range(2):
                    u = 2 * i + par
                    pool.wait_ge(slots_ready, u + 1)
                    for q in range(2):
                        for k in range(K):
                            pool.indirect_dma_start(
                                out=xs_rows[:, :],
                                out_offset=bass.IndirectOffsetOnAxis(ap=slot[:, 2 * u + q, k:k + 1], axis=0),
                                in_=H[:, 2 * u + q, :], in_offset=None).then_inc(scattered, 16)
            pool.wait_ge(ov_ready, 1)
            pool.wait_ge(scattered, 16 * NT * K)
            n = pool.value_load(nov_i[0:1, 0:1], min_val=1, max_val=MAXB)
            with pool.Fori(0, n) as b:
                pool.wait_ge(gcol_ready, b + 1)
                alone(pool, "pool")
                pool.indirect_dma_start(out=xs_rows[:, :], out_offset=bass.IndirectOffsetOnAxis(ap=gcol[:, 0:1], axis=0),
                                        in_=fill[:, 0, :], in_offset=None).then_inc(padded, 16)

            def add_rows(i, s, first):
                e, turn = 4 * i + s, 2 * i + s // 2
                pool.wait_ge(y_ready, e + 1)
                alone(pool, "pool")
                for j in range(2):
                    if not (first and s < 2):
                        pool.wait_ge(added[s % 2][j], 16 * turn)
                        alone(pool, "pool")
                    pool.indirect_dma_start(
                        out=acc[2 * (s % 2) + j][:, :], out_offset=bass.IndirectOffsetOnAxis(ap=toki[:, s, j:j + 1], axis=0),
                        in_=y_sb[:, s, j, :], in_offset=None, compute_op=ALU.add).then_inc(added[s % 2][j], 16)

            for s in range(4):
                add_rows(0, s, True)
            with pool.Fori(1, E // 4) as i:
                for s in range(4):
                    add_rows(i, s, False)
            pool.wait_ge(o_w, 32)
            for q in range(1, 4):
                pool.wait_ge(added[q // 2][q % 2], 16 * (E // 2))
                pool.dma_start(back[q][:, :, :], acc[q][0:T, :].rearrange("(t p) d -> p t d", p=P)).then_inc(early_in, 16)
            pool.wait_ge(added[0][0], 16 * (E // 2))
            with pool.Fori(0, n) as b:
                pool.wait_ge(o_yr, b + 2)
                alone(pool, "pool")
                pool.indirect_dma_start(
                    out=acc[0][:, :], out_offset=bass.IndirectOffsetOnAxis(ap=toki[:, 0, 0:1], axis=0),
                    in_=y_sb[:, 0, 0, :], in_offset=None, compute_op=ALU.add).then_inc(o_add, 16)
                pool.wait_ge(o_add, 16 * b + 16)
                alone(pool, "pool")
            pool.wait_ge(base_ready, NPAIR)
            pool.wait_ge(early_in, 48)
            for q in (1, 2, 3, 0):
                if q == 0:
                    pool.wait_ge(back_in[3], 16)
                pool.tensor_tensor(X[:, 12:16, :], X[:, 12:16, :], back[q][:, 12:16, :], ALU.add).then_inc(sum3_step, 1)
                pool.wait_ge(sum3_step, 4 if q == 0 else q)

        @block.tensor
        def _(pe):
            pe.wait_ge(consts, 1)

            def scores(b, par):
                pe.wait_ge(ctx_in[par], 16 * (b - par) + 32)
                pe.wait_ge(qn_ready, b + 1)
                if later(b):
                    pe.wait_ge(attn_ready, b - 1)
                for e in range(2):
                    m = pe.matmul(psum[:, par, e * D:(e + 1) * D], ctx_s[:, par, e * P:(e + 1) * P], qn[:, par, :],
                                  start=True, stop=True)
                m.then_inc(sc_done, 1)

            def mix(b, par):
                pe.wait_ge(attn_ready, b + 1)
                pe.wait_ge(v_scaled, b + 1)
                if later(b + 1):
                    pe.wait_ge(x1_done, b)
                for e in range(2):
                    m = pe.matmul(psum[:, 2, 0:D], vTs[:, par, e, :], attn[:, par, e, :], start=(e == 0), stop=(e == 1))
                m.then_inc(pv_done, 1)

            def turn(b, par):
                pe.wait_ge(hs_ready, b + 1)
                if later(b + 1):
                    pe.wait_ge(hT_ready, b)
                for k in range(2):
                    m = pe.transpose(psum[:, 3, k * P:(k + 1) * P], hs[:, par, k * P:(k + 1) * P], ident[:, :])
                m.then_inc(hT_full, 1)

            def expand(b, par):
                pe.wait_ge(hT_ready, b + 1)
                if later(b):
                    pe.wait_ge(z_ready, b - 1)
                for c in range(2):
                    for k in range(2):
                        m = pe.matmul(psum[:, 4 + 2 * par + c, :], hTs[:, par, k, :], wsyn[:, k, c * 512:(c + 1) * 512],
                                      start=(k == 0), stop=(k == 1))
                m.then_inc(z_done, 1)

            def first_blocks(b, par):
                if type(b) is int and b == 3:
                    pe.wait_ge(wabs_ready, 1)
                    pe.matmul(psum[:, 7, 0:2], onesf[:, :], wabs[:, :], start=True, stop=True).then_inc(wsum_done, 1)
                    pe.wait_ge(w_ready, 1)
                if there(b - 3):
                    expand(b - 3, 1 - par)
                if there(b + 1):
                    scores(b + 1, 1 - par)
                if there(b):
                    mix(b, par)
                if there(b - 2):
                    turn(b - 2, par)

            pipeline(pe, -1, NT + 2, first_blocks)

            pe.wait_ge(w_ready, 2)
            pe.wait_ge(bad_ready, 1)
            pe.matmul(psum[:, 0, 0:1], onesf[:, :], bad[:, :], start=True, stop=True).then_inc(bad_done, 1)

            def turn_hidden(b, par):
                pe.wait_ge(hid_ready, b + 1)
                if later(b):
                    pe.wait_ge(hidT_ready, b - 1)
                for c in range(8):
                    m = pe.transpose(psum[:, 2 + 2 * par + c // 4, (c % 4) * P:(c % 4 + 1) * P],
                                     hidden[:, par, c * P:(c + 1) * P], ident[:, :])
                m.then_inc(hidT_full, 1)

            def project(b, par):
                pe.wait_ge(hidT_ready, b + 1)
                if later(b):
                    pe.wait_ge(var3_ready, b - 1)
                for c in range(8):
                    m = pe.matmul(psum[:, par, 0:D], hidT[:, par, c * P:(c + 1) * P], wout[:, c, :], start=(c == 0), stop=(c == 7))
                m.then_inc(o_done, 1)

            def turn_q(b, par):
                pe.wait_ge(qs_ready, b + 1)
                if later(b):
                    pe.wait_ge(qT_ready, b - 1)
                for k in range(2):
                    m = pe.transpose(psum[:, 6 + par, k * P:(k + 1) * P], hs[:, par, k * P:(k + 1) * P], ident[:, :])
                m.then_inc(qT_full, 1)

            def second_block(b, par):
                if there(b + 1):
                    turn_hidden(b + 1, 1 - par)
                if there(b):
                    project(b, par)
                if there(b - 3):
                    turn_q(b - 3, 1 - par)

            pipeline(pe, -1, NT + 2, second_block)
            pe.wait_ge(qT_ready, NT)

            def conv(h, par, first):
                pe.wait_ge(kv_ready, h + 1)
                pe.wait_ge(tdiag_ready, h + 1)
                if not first:
                    pe.wait_ge(o3_ready, 2 * h - 2)
                for g in range(2):
                    r = [kv[:, par, m_, 8 * g:8 * g + 8, :].rearrange("p b r -> p (b r)") for m_ in range(2)]
                    w = 8 * NPR
                    pe.matmul(psum[:, 4 * par + g, 0:w], tdiag[:, par, :], r[0], start=True, stop=True)
                    pe.matmul(psum[:, 4 * par + 2 + g, 0:w], toep_s[:, par, 1, :], r[0], start=True, stop=False)
                    m = pe.matmul(psum[:, 4 * par + 2 + g, 0:w], tdiag[:, par, :], r[1], start=False, stop=True)
                m.then_inc(conv_done, 1)

            def sum_queries(h, par):
                pe.wait_ge(halves_ready, h + 1)
                for l in range(2):
                    for s in range(HD // 2):
                        m = pe.matmul(psum[:, 4 * par + l, OS:OS + P], ident[:, :],
                                      prods[:, par, l * 1024:(l + 1) * 1024].rearrange("p (r s) -> p r s", s=HD)[:, :, s],
                                      start=(s == 0), stop=(s == HD // 2 - 1))
                    m.then_inc(osum_done, 1)

            conv(0, 0, True)
            conv(1, 1, True)
            with pe.Fori(1, NH // 2) as i:
                sum_queries(2 * i - 2, 0)
                conv(2 * i, 0, False)
                sum_queries(2 * i - 1, 1)
                conv(2 * i + 1, 1, False)
            sum_queries(NH - 2, 0)
            sum_queries(NH - 1, 1)

            pe.wait_ge(o3_ready, 2 * NH)
            for b in range(NT):
                if b >= 4:
                    pe.wait_ge(x3_done, b - 3)
                for l in range(2):
                    m = pe.transpose(psum[:, b % 4, l * P:(l + 1) * P], OT[:, l, b, :], ident[:, :])
                m.then_inc(o3T_done, 1)

            pe.wait_ge(x3_done, NT)
            pe.wait_ge(gate_in, 16)

            def rank_tile(par, q):
                o = r_log[par][:, 2 * E + E * q:2 * E + E * q + E]
                pe.matmul(o, tri[:, :], mask[:, par, q, :], start=True, stop=False)
                if q == 1:
                    pe.matmul(o, ones[:, :], mask[:, par, 0, :], start=False, stop=False)
                return pe.matmul(o, ones[:, :], macc[:, par, :], start=False, stop=True)

            def logits(u, par):
                pe.wait_ge(h_ready, u + 1)
                for q in range(2):
                    for k in range(2):
                        m = pe.transpose(r_turn[:, k * CAP + q * P:k * CAP + (q + 1) * P],
                                         hst[:, par, q, k * P:(k + 1) * P], ident[:, :])
                m.then_inc(rT_full, 1)
                pe.wait_ge(rT_ready, u + 1)
                for q in range(2):
                    for k in range(2):
                        m = pe.matmul(r_log[par][:, E * q:E * q + E], xT[:, par, k, q * P:(q + 1) * P],
                                      gate_sb[:, k, :], start=(k == 0), stop=(k == 1))
                m.then_inc(logits_done, 1)

            def rank_and_share(u, par):
                pe.wait_ge(mask_ready, u + 1)
                rank_tile(par, 0)
                rank_tile(par, 1).then_inc(rank_done, 1)
                for c, (f0, fw) in enumerate(FS):
                    for g in range(2):
                        for k in range(2):
                            m = pe.matmul(s_up[c][0:fw, g * CAP:(g + 1) * CAP],
                                          wsgu_sb[:, k, g * FSH + f0:g * FSH + f0 + fw],
                                          xT[:, par, k, :], start=(k == 0), stop=(k == 1))
                    m.then_inc(sgu_done, 1)
                pe.wait_ge(shid_ready, 3 * u + 3)
                for j in range(2):
                    for c, (f0, fw) in enumerate(FS):
                        m = pe.matmul(s_y[par][:, j * D:(j + 1) * D], shid[0:fw, par, c, j * P:(j + 1) * P],
                                      wsd_sb[0:fw, c, :], start=(c == 0), stop=(c == 2))
                m.then_inc(sy_done, 1)

            pe.wait_ge(ws_in, 48)
            logits(0, 0)
            with pe.Fori(0, NPAIR // 2 - 1) as i:
                for par in range(2):
                    logits(2 * i + par + 1, 1 - par)
                    rank_and_share(2 * i + par, par)
            logits(NPAIR - 1, 1)
            rank_and_share(NPAIR - 2, 0)
            rank_and_share(NPAIR - 1, 1)

            pe.wait_ge(slots_ready, NPAIR)
            pe.matmul(pT[0][0:E, 0:P], macc[:, 0, :], ones[:, :], start=True, stop=True)
            pe.matmul(pT[0][:, P:P + E], ones[:, :], macc[:, 0, :], start=True, stop=True).then_inc(load_done, 1)
            pe.wait_ge(nb_ready, 1)
            pe.matmul(pT[1][:, 0:E], nb_b[:, :], trii[:, :], start=True, stop=True)
            pe.matmul(pT[1][:, E:2 * E], nb_b[:, :], tri[0:E, 0:E], start=True, stop=True).then_inc(ov_done, 1)
            pe.wait_ge(bval_ready, 1)
            for v in range(3):
                m = pe.matmul(pY[0][:, v * P:(v + 1) * P], bvals[:, v, :], ident[:, :], start=True, stop=True)
            m.then_inc(brow_done, 1)
            pe.wait_ge(ov_ready, 1)

            def transposes(i, s, first):
                e, par = 4 * i + s, s % 2
                pe.wait_ge(xs_in[s], 16 * i + 16)
                if not first:
                    pe.wait_ge(xT_ready, e - 1)
                for j in range(2):
                    for k in range(2):
                        m = pe.transpose(pT[par][:, k * CAP + j * P:k * CAP + (j + 1) * P],
                                         xs_sb[:, s, j, k * P:(k + 1) * P], ident[:, :])
                m.then_inc(xT_full, 1)

            def up(i, s, first):
                e, par = 4 * i + s, s % 2
                pe.wait_ge(w_in[s], 32 * i + 32)
                pe.wait_ge(xT_ready, e + 1)
                if not first:
                    pe.wait_ge(xhid_ready, e - 1)
                for g in range(2):
                    for k in range(2):
                        m = pe.matmul(pA[par][:, g * CAP:(g + 1) * CAP], wgu_sb[:, s, k, g * P:(g + 1) * P],
                                      xT[:, par, k, :], start=(k == 0), stop=(k == 1))
                m.then_inc(guA_done, 1)
                for k in range(2):
                    m = pe.matmul(pC[par][0:GU - 2 * P, 0:CAP], wgu_sb[:, s, k, 2 * P:GU],
                                  xT[:, par, k, :], start=(k == 0), stop=(k == 1))
                m.then_inc(guC_done, 1)

            def down(i, s):
                e, par = 4 * i + s, s % 2
                pe.wait_ge(xhid_ready, e + 1)
                for j in range(2):
                    pe.matmul(pY[par][:, j * D:(j + 1) * D], hid0[:, par, j * P:(j + 1) * P],
                              wd0_sb[:, s, :], start=True, stop=False)
                    m = pe.matmul(pY[par][:, j * D:(j + 1) * D], hid1[:, par, j * P:(j + 1) * P],
                                  wd1_sb[:, s, :], start=False, stop=True)
                m.then_inc(y_done, 1)

            pe.wait_ge(base_ready, NPAIR)
            transposes(0, 0, True)
            transposes(0, 1, True)
            up(0, 0, True)
            transposes(0, 2, False)
            up(0, 1, True)
            down(0, 0)
            transposes(0, 3, False)
            up(0, 2, False)
            down(0, 1)
            with pe.Fori(1, E // 4) as i:
                for s in range(4):
                    transposes(i, s, False)
                    up(i - (s == 0), (s - 1) % 4, False)
                    down(i - (s < 2), (s - 2) % 4)
            up(E // 4 - 1, 3, False)
            down(E // 4 - 1, 2)
            down(E // 4 - 1, 3)

            n = pe.value_load(nov_i[0:1, 0:1], min_val=1, max_val=MAXB)
            with pe.Fori(0, n) as b:
                pe.wait_ge(o_x, 16 * b + 16)
                for k in range(2):
                    m = pe.transpose(pT[0][:, k * P:(k + 1) * P], xs_sb[:, 0, 0, k * P:(k + 1) * P], ident[:, :])
                m.then_inc(o_T, 1)
                pe.wait_ge(o_w, 32 * b + 32)
                pe.wait_ge(o_Tr, b + 1)
                for g in range(2):
                    for k in range(2):
                        pe.matmul(pA[0][:, g * P:(g + 1) * P], wgu_sb[:, 0, k, g * P:(g + 1) * P],
                                  xT[:, 0, k, 0:P], start=(k == 0), stop=(k == 1))
                for k in range(2):
                    m = pe.matmul(pC[0][0:GU - 2 * P, 0:P], wgu_sb[:, 0, k, 2 * P:GU],
                                  xT[:, 0, k, 0:P], start=(k == 0), stop=(k == 1))
                m.then_inc(o_gu, 1)
                pe.wait_ge(o_hid, b + 1)
                pe.matmul(pY[0][:, 0:D], hid0[:, 0, 0:P], wd0_sb[:, 0, :], start=True, stop=False)
                pe.matmul(pY[0][:, 0:D], hid1[:, 0, 0:P], wd1_sb[:, 0, :], start=False, stop=True).then_inc(o_y, 1)

        @block.scalar
        def _(act):
            for dst, src, n in ((gates, gates_in, 4), (bsyn_b, bsyn, N), (bout_b, bout, D), (gam_b, gamma, D),
                                (bet_b, beta, D), (D_b, ssm_D, NH)):
                act.dma_start(dst[:, :], bc(src, n)).then_inc(small_in, 16)
            act.wait_ge(small_in, 96)
            act.activation(tg[:, :], gates[:, :], ACT.Tanh).then_inc(tg_ready, 1)

            def soft(b, par):
                act.wait_ge(smax_ready, b + 1)
                if later(b):
                    act.wait_ge(pv_done, b - 1)
                for e in range(2):
                    m = act.activation(attn[:, par, e, :], psum[:, par, e * D:(e + 1) * D], ACT.Exp,
                                       bias=nsmax[:, par, e:e + 1], scale=1.0 / 16, accum_out=asum[:, par, e:e + 1])
                m.then_inc(attn_ready, 1)

            def evac_h(b, par):
                act.wait_ge(hT_full, b + 1)
                if later(b):
                    act.wait_ge(z_done, b - 1)
                act.activation(hTs[:, par], psum[:, 3, 0:D].rearrange("p (k c) -> p k c", k=2), ACT.Copy).then_inc(hT_ready, 1)

            def first_blocks(b, par):
                if there(b):
                    soft(b, par)
                if there(b - 2):
                    evac_h(b - 2, par)

            pipeline(act, 0, NT + 1, first_blocks)

            act.wait_ge(z_ready, NT)
            for r in range(ROUNDS):
                act.wait_ge(thr_ready, r + 1)
                with act.Fori(NTD, NT) as t:
                    m = act.activation(ajunk[:, t - NTD, :], z[:, t, :], ACT.Sign, bias=nthr[:, bass.ds(t, 1)],
                                       accum_out=cnt[:, bass.ds(t, 1)])
                    m.then_inc(cnt_done, 1)
                act.wait_ge(cnt_done, (NT - NTD) * (r + 1))

            act.wait_ge(thr_ready, ROUNDS + 1)
            for half in range(2):
                with act.Fori(NTD, NT) as t:
                    if half == 0:
                        m = act.activation(junk[:, t - NTD, :], z[:, t, :], ACT.Relu, bias=hib[:, bass.ds(t, 1)], scale=-BIG)
                    else:
                        m = act.activation(junk[:, t - NTD, :], junk[:, t - NTD, :], ACT.Sign, accum_out=below[:, bass.ds(t, 1)])
                    m.then_inc(below_done if half else above_done, 1)
                if half == 0:
                    act.wait_ge(above_done, NT - NTD)

            def evac_hidden(b, par):
                act.wait_ge(hidT_full, b + 1)
                if later(b):
                    act.wait_ge(o_done, b - 1)
                act.activation(hidT[:, par, :].rearrange("p (a n) -> p a n", a=2), psum[:, 2 + 2 * par:4 + 2 * par, :],
                               ACT.Copy).then_inc(hidT_ready, 1)

            def evac_q(b, par):
                act.wait_ge(qT_full, b + 1)
                act.activation(qT[:, :, b, :], psum[:, 6 + par, 0:D].rearrange("p (k c) -> p k c", k=2), ACT.Copy).then_inc(qT_ready, 1)

            def second_block(b, par):
                if there(b + 1):
                    evac_hidden(b + 1, 1 - par)
                if there(b - 3):
                    evac_q(b - 3, 1 - par)

            pipeline(act, -1, NT + 2, second_block)

            def keep_sums(h, par):
                for l in range(2):
                    act.wait_ge(osum_done, 2 * h + l + 1)
                    act.activation(OT[:, l, :, bass.ds(h * HD, HD)],
                                       psum[:, 4 * par + l, OS:OS + P].rearrange("p (b j) -> p b j", j=HD), ACT.Copy).then_inc(o3_ready, 1)

            with act.Fori(0, NH // 2) as i:
                keep_sums(2 * i, 0)
                keep_sums(2 * i + 1, 1)

            def evac_x(u, par):
                act.wait_ge(rT_full, u + 1)
                act.activation(xT[:, par], r_turn[:, :].rearrange("p (k c) -> p k c", k=2), ACT.Copy).then_inc(rT_ready, 1)

            def exponents(u, par):
                act.wait_ge(negmax_ready, u + 1)
                for q in range(2):
                    act.activation(e64[:, par, q], lg[:, par, q], ACT.Exp, bias=negmax[:, par, q:q + 1],
                                   accum_out=sum64[:, par, q:q + 1])
                    m = act.activation(e6[:, par, q], top8[:, par, q, 0:K], ACT.Exp, bias=negmax[:, par, q:q + 1])
                m.then_inc(exp_done, 1)

            def shared_silu(u, par):
                for c, (f0, fw) in enumerate(FS):
                    act.wait_ge(sgu_done, 3 * u + c + 1)
                    act.activation(ssil[0:fw, par, c], s_up[c][0:fw, 0:CAP], ACT.Silu).then_inc(ssilu_done, 1)

            evac_x(0, 0)
            exponents(0, 0)
            with act.Fori(0, NPAIR // 2 - 1) as i:
                for par in range(2):
                    evac_x(2 * i + par + 1, 1 - par)
                    shared_silu(2 * i + par, par)
                    exponents(2 * i + par + 1, 1 - par)
            evac_x(NPAIR - 1, 1)
            shared_silu(NPAIR - 2, 0)
            exponents(NPAIR - 1, 1)
            shared_silu(NPAIR - 1, 1)

            def evac(e, par, first):
                act.wait_ge(xT_full, e + 1)
                if not first:
                    act.wait_ge(guC_done, e - 1)
                act.activation(xT[:, par], pT[par][:, :].rearrange("p (k c) -> p k c", k=2), ACT.Copy).then_inc(xT_ready, 1)

            def silu(e, par, first):
                act.wait_ge(guA_done, e + 1)
                if not first:
                    act.wait_ge(xhid_ready, e - 1)
                act.activation(sil0[:, par], pA[par][:, 0:CAP], ACT.Silu).then_inc(silA_done, 1)
                act.wait_ge(guC_done, e + 1)
                act.activation(sil1[:, par], pC[par][0:F1, 0:CAP], ACT.Silu).then_inc(silC_done, 1)

            evac(0, 0, True)
            evac(1, 1, True)
            silu(0, 0, True)
            evac(2, 0, False)
            silu(1, 1, True)
            evac(3, 1, False)
            silu(2, 0, False)
            with act.Fori(1, E // 2 - 1) as i:
                evac(2 * i + 2, 0, False)
                silu(2 * i + 1, 1, False)
                evac(2 * i + 3, 1, False)
                silu(2 * i + 2, 0, False)
            silu(E - 1, 1, False)
            act.wait_ge(ov_ready, 1)
            n = act.value_load(nov_i[0:1, 0:1], min_val=1, max_val=MAXB)
            with act.Fori(0, n) as b:
                act.wait_ge(o_T, b + 1)
                act.activation(xT[:, 0, :, 0:P], pT[0][:, 0:CAP].rearrange("p (k c) -> p k c", k=2), ACT.Copy).then_inc(o_Tr, 1)
                act.wait_ge(o_gu, b + 1)
                act.activation(sil0[:, 0, 0:P], pA[0][:, 0:P], ACT.Silu)
                act.activation(sil1[:, 0, 0:P], pC[0][0:F1, 0:P], ACT.Silu).then_inc(o_silu, 1)

        @block.vector
        def _(dve):
            v = {"at": 0, "k": 0}

            def link(ins):
                v["k"] += 1
                ins.then_inc(v_step, 1)
                dve.wait_ge(v_step, v["at"] + v["k"])

            def tiles(lo_, hi_, per, body):
                start = v["at"] + v["k"]
                with dve.Fori(lo_, hi_) as i:
                    v["at"], v["k"] = start + (i - lo_) * per, 0
                    body(i)
                    assert v["k"] == per, (v["k"], per)
                v["at"], v["k"] = start + (hi_ - lo_) * per, 0

            def run(first, last, body):
                with dve.Fori(first, last) as t:
                    body(t).then_inc(v_step, 1)
                v["k"] += last - first
                dve.wait_ge(v_step, v["at"] + v["k"])

            def moments(src, t, signal):
                alone(dve, "dve")
                link(dve.bn_stats(stats[:, 0, :], src))
                alone(dve, "dve")
                link(dve.bn_aggr(mvt[:, 0, :], stats[:, 0, :]))
                dve.tensor_tensor(mv[:, t, :], mvt[:, 0, :], eps2[:, :], ALU.add).then_inc(signal, 1)

            def input_moments(c):
                dve.wait_ge(x_in[c], 16)
                alone(dve, "dve")
                run(4 * c, 4 * c + 4, lambda t: dve.bn_stats(stats[:, t, :], X[:, t, :]))
                alone(dve, "dve")
                for t in range(4 * c, 4 * c + 4):
                    m = dve.bn_aggr(mvt[:, t, :], stats[:, t, :])
                link(m)
                dve.tensor_tensor(mv[:, 4 * c:4 * c + 4, :], mvt[:, 4 * c:4 * c + 4, :], eps2[:, None, :].to_broadcast([P, 4, 2]),
                                  ALU.add).then_inc(var_ready, 1)

            dve.wait_ge(consts, 1)
            input_moments(0)
            dve.wait_ge(small_in, 96)
            dve.wait_ge(tg_ready, 1)
            dve.tensor_scalar(gam_b[:, :], gam_b[:, :], tg[:, 1:2], None, ALU.mult)
            dve.tensor_scalar(bet_b[:, :], bet_b[:, :], tg[:, 1:2], None, ALU.mult)

            def weight_scales():
                dve.wait_ge(wraw_in, 32)
                dve.tensor_reduce(wabs[:, 0:1], wraw[:, 0:2, :], AX.XY, ALU.add, apply_absolute_value=True)
                dve.tensor_reduce(wabs[:, 1:2], wraw[:, 2:4, :], AX.XY, ALU.add, apply_absolute_value=True).then_inc(wabs_ready, 1)
                dve.wait_ge(wsum_done, 1)
                link(dve.tensor_scalar(wsc[:, :], psum[:, 7, 0:2], 1.0 / (D * N), None, ALU.mult))
                link(dve.tensor_scalar(wcut[:, :], wsc[:, :], 1e-8, 0.5, ALU.add, ALU.mult))
                link(dve.tensor_scalar(wneg[:, :], wcut[:, :], -1.0, None, ALU.mult))
                link(dve.tensor_scalar(spread[:, 0:1], wsc[:, 0:1], SIG, None, ALU.mult))
                dve.tensor_scalar(spread[:, 1:2], spread[:, 0:1], 1.0 / DENS, None, ALU.mult)

            def ternary(w):
                raw, signs = wraw[:, 2 * w:2 * w + 2, :], wt[:, 2 * w:2 * w + 2, :]
                link(dve.tensor_scalar(signs, raw, wneg[:, w:w + 1], None, ALU.is_lt))
                dve.scalar_tensor_tensor(signs, raw, wcut[:, w:w + 1], signs, ALU.is_gt, ALU.subtract).then_inc(w_ready, 1)

            def query(b, par):
                if type(b) is int and b % 4 == 0 and b < NT - 3:
                    dve.wait_ge(rstd_ready, b // 4 + 1)
                if later(b):
                    dve.wait_ge(sc_done, b - 1)
                dve.tensor_scalar(qn[:, par, :], X[:, b, :], mv[:, b, 0:1], rstd[:, bass.ds(b, 1)], ALU.subtract, ALU.mult).then_inc(qn_ready, 1)

            def highest(b, par):
                dve.wait_ge(sc_done, b + 1)
                link(dve.tensor_reduce(smax[:, :], psum[:, par, :].rearrange("p (e d) -> p e d", e=2), AX.X, ALU.max))
                dve.tensor_scalar(nsmax[:, par, :], smax[:, :], -1.0 / 16, None, ALU.mult).then_inc(smax_ready, 1)

            def scale_v(b, par):
                dve.wait_ge(attn_ready, b + 1)
                dve.wait_ge(ctx_in[par], 16 * (b - par) + 32)
                link(dve.reciprocal(rsum[:, :], asum[:, par, :]))
                for e in range(2):
                    m = dve.tensor_scalar(vTs[:, par, e, :], ctxT_s[:, par, e, :], rsum[:, e:e + 1], None, ALU.mult)
                m.then_inc(v_scaled, 1)

            def add1(b, par):
                dve.wait_ge(pv_done, b + 1)
                m = dve.scalar_tensor_tensor(X[:, b, :], psum[:, 2, 0:D], tg[:, 0:1], X[:, b, :], ALU.mult, ALU.add)
                m.then_inc(x1_done, 1)
                dve.wait_ge(x1_done, b + 1)
                moments(X[:, b, :], b, var2_ready)

            def norm_h(b, par):
                dve.wait_ge(rstd2_ready, b + 1)
                if later(b):
                    dve.wait_ge(hT_full, b - 1)
                    dve.wait_ge(h2b_done, b - 1)
                dve.tensor_scalar(hs[:, par, :], X[:, b, :], mv[:, b, 0:1], rstd[:, bass.ds(b, 1)], ALU.subtract, ALU.mult).then_inc(hs_ready, 1)

            def keep_z(b, par):
                dve.wait_ge(z_done, b + 1)
                dve.scalar_tensor_tensor(z[:, b, :].rearrange("p (a n) -> p a n", a=2), psum[:, 4 + 2 * par:6 + 2 * par, :], wsc[:, 0:1],
                                         bsyn_b[:, :].rearrange("p (a n) -> p a n", a=2), ALU.mult, ALU.add).then_inc(z_ready, 1)

            def first_blocks(b, par):
                if type(b) is int and 0 <= b < 4:
                    if b:
                        input_moments(b)
                    if b == 3:
                        weight_scales()
                        ternary(0)
                        dve.wait_ge(rstd_ready, 4)
                if type(b) is int and b == 5:
                    ternary(1)
                if there(b):
                    highest(b, par)
                if there(b - 1):
                    add1(b - 1, 1 - par)
                if there(b - 4):
                    keep_z(b - 4, par)
                if there(b):
                    scale_v(b, par)
                if there(b + 2):
                    query(b + 2, par)
                if there(b - 2):
                    norm_h(b - 2, par)

            def dve_pipeline(first, last, per, body):
                for b in range(first, EARLY):
                    body(b, b % 2)

                def pair(i):
                    body(2 * i, 0)
                    body(2 * i + 1, 1)

                tiles(EARLY // 2, LATE // 2, per, pair)
                for b in range(LATE, last + 1):
                    body(b, b % 2)

            dve_pipeline(-2, NT + 3, 8, first_blocks)
            dve.wait_ge(z_ready, NT)

            link(dve.memset(thr[:, :], 1.2817))
            link(dve.tensor_scalar(thr[:, :], thr[:, :], spread[:, 0:1], None, ALU.mult))
            dve.tensor_scalar(nthr[:, :], thr[:, :], -1.0, None, ALU.mult).then_inc(thr_ready, 1)

            def count(t, at):
                return dve.tensor_scalar(junk[:, t, :], z[:, t, :], at[:, bass.ds(t, 1)], 0.0, ALU.is_ge, ALU.add,
                                         accum_out=cnt[:, bass.ds(t, 1)])

            for r in range(ROUNDS):
                with dve.Fori(0, NTD) as t:
                    count(t, thr).then_inc(l_step, 1)
                dve.wait_ge(l_step, NTD * (r + 1))
                dve.wait_ge(cnt_done, (NT - NTD) * (r + 1))
                link(dve.tensor_scalar(cnt[:, NTD:NT], cnt[:, NTD:NT], 0.5, N / 2.0, ALU.mult, ALU.add))
                dve.tensor_scalar(up[:, :], cnt[:, :], float(TOPK), None, ALU.is_gt)
                last = dve.tensor_scalar(dn[:, :], cnt[:, :], float(TOPK), None, ALU.is_le)
                if r == 0:
                    link(dve.tensor_scalar(t1[:, :], cnt[:, :], FAR - AIM, spread[:, 1:2], ALU.add, ALU.mult))
                    link(dve.tensor_scalar(t2[:, :], cnt[:, :], -FAR - AIM, spread[:, 1:2], ALU.add, ALU.mult))
                    dve.tensor_tensor(hi[:, :], thr[:, :], t1[:, :], ALU.add)
                    dve.tensor_tensor(lo[:, :], thr[:, :], t2[:, :], ALU.add)
                    dve.memset(chi[:, :], AIM - FAR)
                    link(dve.memset(clo[:, :], AIM + FAR))
                else:
                    link(last)
                dve.copy_predicated(lo[:, :], up[:, :], thr[:, :])
                dve.copy_predicated(clo[:, :], up[:, :], cnt[:, :])
                dve.copy_predicated(hi[:, :], dn[:, :], thr[:, :])
                link(dve.copy_predicated(chi[:, :], dn[:, :], cnt[:, :]))
                if r < ROUNDS - 1:
                    dve.tensor_tensor(t1[:, :], clo[:, :], chi[:, :], ALU.subtract)
                    dve.tensor_tensor(t2[:, :], hi[:, :], lo[:, :], ALU.subtract)
                    link(dve.tensor_scalar(t3[:, :], clo[:, :], -float(AIM), None, ALU.add))
                    link(dve.reciprocal(t1[:, :], t1[:, :]))
                    link(dve.tensor_tensor(t2[:, :], t2[:, :], t3[:, :], ALU.mult))
                    link(dve.tensor_tensor(t2[:, :], t2[:, :], t1[:, :], ALU.mult))
                    link(dve.tensor_tensor(t2[:, :], t2[:, :], lo[:, :], ALU.add))
                    link(dve.tensor_tensor(t2[:, :], t2[:, :], hi[:, :], ALU.min))
                    link(dve.tensor_tensor(thr[:, :], t2[:, :], lo[:, :], ALU.max))
                    dve.tensor_scalar(nthr[:, :], thr[:, :], -1.0, None, ALU.mult).then_inc(thr_ready, 1)
                else:
                    dve.tensor_copy(m9[:, :, 0], hi[:, :])
                    dve.tensor_scalar(hib[:, :], hi[:, :], BIG, None, ALU.mult).then_inc(thr_ready, 1)
            def mask_tile(t):
                if t >= 4:
                    dve.wait_ge(max_done, t - 3)
                dve.scalar_tensor_tensor(hh[:, t % 4, :], z[:, t, :], hi[:, t:t + 1], z[:, t, :],
                                         ALU.is_lt, ALU.mult).then_inc(masked, 1)

            mask_tile(0)
            for t in range(NT):
                if t + 1 < NT:
                    mask_tile(t + 1)
                dve.wait_ge(masked, t + 1)
                alone(dve, "dve")
                dve.max(m9[:, t, 1:9], hh[:, t % 4, :]).then_inc(max_done, 1)
            dve.wait_ge(max_done, NT)
            dve.wait_ge(below_done, NT - NTD)
            link(dve.tensor_scalar(chi[:, NTD:NT], below[:, NTD:NT], -1.0, float(N), ALU.mult, ALU.add))
            dve.tensor_scalar(t1[:, :], chi[:, :], -1.0, float(TOPK), ALU.mult, ALU.add)
            dve.tensor_scalar(t2[:, :], chi[:, :], float(NEAR), None, ALU.is_ge)
            link(dve.tensor_scalar(t3[:, :], chi[:, :], float(TOPK), None, ALU.is_le))
            link(dve.tensor_tensor(t2[:, :], t2[:, :], t3[:, :], ALU.mult))
            link(dve.tensor_reduce(bad[:, :], t2[:, :], AX.X, ALU.min))
            dve.tensor_scalar(bad[:, :], bad[:, :], -1.0, 1.0, ALU.mult, ALU.add).then_inc(bad_ready, 1)
            link(dve.tensor_tensor(m9s[:, :, :], iota9[:, None, :].to_broadcast([P, NT, 9]), t1[:, :, None].to_broadcast([P, NT, 9]), ALU.is_equal))
            link(dve.tensor_tensor(m9s[:, :, :], m9s[:, :, :], m9[:, :, :], ALU.mult))
            link(dve.tensor_reduce(thr[:, :], m9s[:, :, :], AX.X, ALU.add))
            dve.wait_ge(bad_done, 1)
            link(dve.tensor_copy(bad_i[:, :], psum[:, 0, 0:1]))
            n_bad = dve.value_load(bad_i[0:1, 0:1], min_val=0, max_val=P)
            with dve.If(n_bad > 0):
                with dve.Fori(0, NT) as t:
                    steps = 2 * ((TOPK - 1) // 8) + 3
                    k = 1
                    dve.tensor_copy(hidden[:, 0, :], z[:, t, :]).then_inc(p_step, 1)
                    dve.wait_ge(p_step, 2 + t * steps + k)
                    for q in range((TOPK - 1) // 8):
                        alone(dve, "dve")
                        dve.max(m8[:, 0, :], hidden[:, 0, :]).then_inc(p_step, 1)
                        k += 1
                        dve.wait_ge(p_step, 2 + t * steps + k)
                        alone(dve, "dve")
                        dve.match_replace(hidden[:, 0, :], m8[:, 0, :], hidden[:, 0, :], -3e38).then_inc(p_step, 1)
                        k += 1
                        dve.wait_ge(p_step, 2 + t * steps + k)
                    alone(dve, "dve")
                    dve.max(m8[:, 0, :], hidden[:, 0, :]).then_inc(p_step, 1)
                    k += 1
                    dve.wait_ge(p_step, 2 + t * steps + k)
                    dve.tensor_copy(thr[:, bass.ds(t, 1)], m8[:, 0, (TOPK - 1) % 8:(TOPK - 1) % 8 + 1]).then_inc(p_step, 1)
                    k += 1
                    assert k == steps
                    dve.wait_ge(p_step, 2 + t * steps + k)
            link(dve.tensor_scalar(thr[:, :], thr[:, :], 0.0, None, ALU.max))

            def make_hidden(b, par):
                if later(b):
                    dve.wait_ge(hidT_full, b - 1)
                dve.scalar_tensor_tensor(hidden[:, par, :], z[:, b, :], thr[:, bass.ds(b, 1)], z[:, b, :], ALU.is_ge, ALU.mult).then_inc(hid_ready, 1)

            def residual(b, par):
                dve.wait_ge(o_done, b + 1)
                dve.wait_ge(h2b_done, b + 1)
                link(dve.scalar_tensor_tensor(H2[:, b, :], psum[:, par, 0:D], wsc[:, 1:2], H2[:, b, :], ALU.mult, ALU.add))
                moments(H2[:, b, :], b, var3_ready)

            def add2(b):
                dve.wait_ge(rstd3_ready, b + 1)
                link(dve.scalar_tensor_tensor(H2[:, b, :], H2[:, b, :], mv[:, b, 0:1], gam_b[:, :], ALU.subtract, ALU.mult))
                link(dve.scalar_tensor_tensor(X[:, b, :], H2[:, b, :], rstd[:, bass.ds(b, 1)], X[:, b, :], ALU.mult, ALU.add))
                moments(X[:, b, :], b, var4_ready)

            def query3(b, par):
                dve.wait_ge(rstd4_ready, b + 1)
                if later(b):
                    dve.wait_ge(qT_full, b - 1)
                dve.tensor_scalar(hs[:, par, :], X[:, b, :], mv[:, b, 0:1], rstd[:, bass.ds(b, 1)], ALU.subtract, ALU.mult).then_inc(qs_ready, 1)

            def second_block(b, par):
                if there(b + 2):
                    make_hidden(b + 2, par)
                if there(b):
                    residual(b, par)
                if there(b - 1):
                    add2(b - 1)
                if there(b - 2):
                    query3(b - 2, par)

            dve_pipeline(-2, NT + 1, 14, second_block)

            def diag(h, par, i, first):
                dve.wait_ge(head_in[par], 32 * i + 32)
                if not first:
                    dve.wait_ge(conv_done, h - 1)
                dve.scalar_tensor_tensor(tdiag[:, par, :], ident[:, :], D_b[:, bass.ds(h, 1)], toep_s[:, par, 0, :], ALU.mult, ALU.add).then_inc(tdiag_ready, 1)

            def times_q(h, par):
                dve.wait_ge(conv_done, h + 1)
                R = prods[:, par, :].rearrange("p (g b j s) -> p g b j s", g=4, b=8, j=HD)
                Y = psum[:, 4 * par:4 * par + 4, 0:8 * NPR].rearrange("p g (b r) -> p g b r", r=NPR)
                at = 0
                for d in range(HD):
                    n = HD - d
                    y = Y[:, :, :, at:at + n]
                    q0 = qT[:, :, :, bass.ds(h * HD, n)].rearrange("p l (g b) i -> p (l g) b i", g=2)
                    m = dve.tensor_tensor(R[:, :, :, d:HD, d], y, q0, ALU.mult)
                    if d:
                        q1 = qT[:, :, :, bass.ds(h * HD + d, n)].rearrange("p l (g b) i -> p (l g) b i", g=2)
                        m = dve.tensor_tensor(R[:, :, :, 0:n, HD - d], y, q1, ALU.mult)
                    at += n
                m.then_inc(prod_done, 1)
                dve.wait_ge(prod_done, h + 1)
                halves = prods[:, par, :].rearrange("p (r s) -> p r s", s=HD)
                dve.tensor_tensor(halves[:, :, 0:HD // 2], halves[:, :, 0:HD // 2], halves[:, :, HD // 2:HD], ALU.add).then_inc(halves_ready, 1)

            dve.wait_ge(qT_ready, NT)
            diag(0, 0, 0, True)
            diag(1, 1, 0, True)
            times_q(0, 0)
            with dve.Fori(1, NH // 2) as i:
                diag(2 * i, 0, i, False)
                times_q(2 * i - 1, 1)
                diag(2 * i + 1, 1, i, False)
                times_q(2 * i, 0)
            times_q(NH - 1, 1)

            def x3_stats(b):
                dve.wait_ge(x3_done, b + 1)
                alone(dve, "dve")
                dve.bn_stats(stats[:, b, :], X[:, b, :]).then_inc(stats_done, 1)

            def x3_moments(g):
                dve.wait_ge(stats_done, 4 * g + 4)
                alone(dve, "dve")
                for t in range(4 * g, 4 * g + 4):
                    m = dve.bn_aggr(mvt[:, t, :], stats[:, t, :])
                link(m)
                dve.tensor_tensor(mv[:, 4 * g:4 * g + 4, :], mvt[:, 4 * g:4 * g + 4, :], eps2[:, None, :].to_broadcast([P, 4, 2]),
                                  ALU.add).then_inc(var5_ready, 1)

            for b in range(NT):
                dve.wait_ge(o3T_done, b + 1)
                dve.scalar_tensor_tensor(X[:, b, :], psum[:, b % 4, 0:D], tg[:, 2:3], X[:, b, :], ALU.mult, ALU.add).then_inc(x3_done, 1)
                if b:
                    x3_stats(b - 1)
                if b % 4 == 0 and b:
                    x3_moments(b // 4 - 1)
            x3_stats(NT - 1)
            x3_moments(3)
            dve.wait_ge(rstd5_ready, 1)


            dve.wait_ge(c_done, 2)
            LINKS = 22
            def normalise(u, par):
                for q in range(2):
                    dve.tensor_scalar(hst[:, par, q, :], X[:, 2 * u + q, :], mv[:, 2 * u + q, 0:1], rstd[:, bass.ds(2 * u + q, 1)], ALU.subtract, ALU.mult)
                    m = dve.tensor_scalar(H[:, 2 * u + q, 0:D], X[:, 2 * u + q, :], mv[:, 2 * u + q, 0:1], rstd[:, bass.ds(2 * u + q, 1)], ALU.subtract, ALU.mult)
                m.then_inc(h_ready, 1)

            def choose(u, par):
                dve.wait_ge(logits_done, u + 1)
                link(dve.tensor_copy(lg[:, par], r_log[par][:, 0:2 * E].rearrange("p (q e) -> p q e", q=2)))
                alone(dve, "dve")
                dve.max(top8[:, par, 0, :], lg[:, par, 0, :])
                link(dve.max(top8[:, par, 1, :], lg[:, par, 1, :]))
                dve.tensor_scalar(negmax[:, par, :], top8[:, par, :, 0], -1.0, None, ALU.mult).then_inc(negmax_ready, 1)
                dve.max_index(idx8[:, par, 0, :], top8[:, par, 0, :], lg[:, par, 0, :])
                link(dve.max_index(idx8[:, par, 1, :], top8[:, par, 1, :], lg[:, par, 1, :]))
                link(dve.tensor_copy(idxf[:, par], idx8[:, par]))
                for q in range(2):
                    dve.tensor_copy(H[:, 2 * u + q, CE:CE + K], idxf[:, par, q, 0:K])
                for q in range(2):
                    m = dve.tensor_tensor(oh[:, par, q], iota_e[:, None, :].to_broadcast([P, K, E]),
                                          idxf[:, par, q, 0:K, None].to_broadcast([P, K, E]), ALU.is_equal)
                link(m)
                dve.tensor_reduce(mask[:, par], oh[:, par].rearrange("p q k e -> p q e k"), AX.X, ALU.max).then_inc(mask_ready, 1)

            def place(u, par):
                dve.wait_ge(exp_done, u + 1)
                link(dve.tensor_reduce(den[:, :, 0], e6[:, par], AX.X, ALU.add))
                link(dve.scalar_tensor_tensor(den[:, :, 1], sum64[:, par], 1e-20, den[:, :, 0], ALU.mult, ALU.add))
                link(dve.reciprocal(den[:, :, 0], den[:, :, 1]))
                for q in range(2):
                    dve.tensor_scalar(H[:, 2 * u + q, CW:CW + K], e6[:, par, q, :], den[:, q, 0:1], tg[:, 3:4], ALU.mult, ALU.mult)
                dve.wait_ge(rank_done, u + 1)
                dve.tensor_tensor(msum[:, :], mask[:, par, 0, :], mask[:, par, 1, :], ALU.add)
                link(dve.tensor_tensor(posr[:, :, :], r_log[par][:, 2 * E:4 * E].rearrange("p (q e) -> p q e", q=2),
                                       iota_row[:, None, :].to_broadcast([P, 2, E]), ALU.add))
                dve.tensor_tensor(macc[:, 1 - par, :], macc[:, par, :], msum[:, :], ALU.add)
                for q in range(2):
                    m = dve.tensor_tensor(prod[:, q], oh[:, par, q], posr[:, q, None, :].to_broadcast([P, K, E]), ALU.mult)
                link(m)
                link(dve.tensor_reduce(slotf[:, :, :], prod[:, :, :, :], AX.X, ALU.add))
                for q in range(2):
                    m = dve.tensor_copy(slot[:, 2 * u + q, :], slotf[:, q, :])
                m.then_inc(slots_ready, 1)

            def shared_hidden(u, par):
                for c, (f0, fw) in enumerate(FS):
                    dve.wait_ge(ssilu_done, 3 * u + c + 1)
                    dve.tensor_tensor(shid[0:fw, par, c], ssil[0:fw, par, c], s_up[c][0:fw, CAP:2 * CAP], ALU.mult).then_inc(shid_ready, 1)

            def shared_out(u, par):
                dve.wait_ge(sy_done, u + 1)
                for j in range(2):
                    m = dve.scalar_tensor_tensor(X[:, 2 * u + j, :], s_y[par][:, j * D:(j + 1) * D], tg[:, 3:4], X[:, 2 * u + j, :], ALU.mult, ALU.add)
                m.then_inc(base_ready, 1)

            def route_pair(i, last):
                for par in range(2):
                    u = 2 * i + par
                    place(u, par)
                    if not last:
                        normalise(u + 2, par)
                    shared_hidden(u, par)
                    if not (last and par):
                        choose(u + 1, 1 - par)
                    shared_out(u, par)

            normalise(0, 0)
            normalise(1, 1)
            choose(0, 0)
            dve.wait_ge(rstd5_ready, 4)
            tiles(0, NPAIR // 2 - 1, LINKS, lambda i: route_pair(i, False))
            route_pair(NPAIR // 2 - 1, True)

            dve.wait_ge(load_done, 1)
            link(dve.tensor_copy(cnt_f[:, :], pT[0][0:E, 0:P]))
            dve.tensor_copy(ov_c[:, 0, :], pT[0][:, P:P + E])
            link(dve.tensor_scalar(nb_i[:, :], cnt_f[:, :], float(-(CAP + 1 - P)), 0.0, ALU.add, ALU.max))
            link(dve.tensor_scalar(nb_j[:, :], nb_i[:, :], 7, None, ALU.logical_shift_right))
            dve.tensor_copy(nb_b[:, :], nb_j[:, :]).then_inc(nb_ready, 1)
            dve.wait_ge(ov_done, 1)
            link(dve.tensor_copy(ov_c[:, 1, :], pT[1][:, E:2 * E]))
            link(dve.tensor_scalar(ov_w[:, 0, :], pT[1][:, 0:E], pid[:, 0:1], 0.0, ALU.is_le, ALU.add, accum_out=ov_s[:, 0:1]))
            link(dve.tensor_scalar(ov_s[:, 1:2], ov_s[:, 0:1], float(E - 1), None, ALU.min))
            link(dve.scalar_tensor_tensor(ov_w[:, 1, :], iota_e[:, :], ov_s[:, 1:2], ov_c[:, 0, :], ALU.is_equal, ALU.mult, accum_out=ov_s[:, 2:3]))
            link(dve.scalar_tensor_tensor(ov_w[:, 2, :], iota_e[:, :], ov_s[:, 1:2], ov_c[:, 1, :], ALU.is_equal, ALU.mult, accum_out=ov_s[:, 3:4]))
            dve.tensor_scalar(ov_s[:, 5:6], ov_s[:, 1:2], float(T), None, ALU.mult)
            link(dve.tensor_scalar(ov_s[:, 4:5], ov_s[:, 3:4], pid[:, 0:1], -float(P), ALU.subtract, ALU.mult))
            link(dve.tensor_scalar(ov_s[:, 6:7], ov_s[:, 4:5], ov_s[:, 5:6], float(CAP), ALU.add, ALU.add))
            link(dve.tensor_scalar(ov_s[:, 8:9], ov_s[:, 2:3], -1.0, 0.0, ALU.add, ALU.max))
            link(dve.tensor_tensor(ov_s[:, 7:8], ov_s[:, 8:9], ov_s[:, 5:6], ALU.add))
            for r, c in enumerate((6, 7, 1)):
                m = dve.tensor_scalar(bvals[:, r, :], ident[:, :], 0.0, ov_s[:, c:c + 1], ALU.mult, ALU.add)
            m.then_inc(bval_ready, 1)
            dve.wait_ge(brow_done, 1)
            link(dve.tensor_copy(rows_f[:, :, :], pY[0][:, 0:3 * P].rearrange("p (v b) -> p v b", v=3)))
            link(dve.tensor_scalar(rows_f[:, 0, :], rows_f[:, 0, :], pid[:, 0:1], None, ALU.add))
            dve.tensor_tensor(gvalid[:, :], rows_f[:, 0, :], rows_f[:, 1, :], ALU.is_le)
            link(dve.tensor_scalar(gpad[:, :], rows_f[:, 0, :], dump[:, 0:1], -1.0, ALU.subtract, ALU.mult))
            link(dve.tensor_tensor(gpad[:, :], gpad[:, :], gvalid[:, :], ALU.mult))
            link(dve.tensor_tensor(gidx[:, :], gpad[:, :], rows_f[:, 0, :], ALU.add))
            dve.tensor_copy(eb_i[:, 0, :], rows_f[0:1, 2, :])
            dve.tensor_copy(eb_i[:, 1, :], rows_f[0:1, 0, :])
            dve.tensor_scalar(nov_i[:, :], pT[1][:, E - 1:E], 1.0, None, ALU.max).then_inc(ov_ready, 1)
            dve.wait_ge(ov_ready, 1)
            n = dve.value_load(nov_i[0:1, 0:1], min_val=1, max_val=MAXB)

            dve.memset(ovcol[:, 1:2], 0.0).then_inc(o_yr, 1)
            with dve.Fori(0, n) as b:
                dve.tensor_copy(gcol[:, :], gidx[:, bass.ds(b, 1)]).then_inc(gcol_ready, 1)
                dve.wait_ge(padded, 16 * b + 16)
                alone(dve, "dve")

            def weights(i, s, first):
                e, par, turn = 4 * i + s, s % 2, 2 * i + s // 2
                dve.wait_ge(xs_in[s], 16 * i + 16)
                if not first:
                    dve.wait_ge(added[par][0], 16 * turn - 16)
                    dve.wait_ge(added[par][1], 16 * turn - 16)
                for j in range(2):
                    dve.scalar_tensor_tensor(wsel[:, s, j, :], xs_sb[:, s, j, CE:CE + K], iota_e[:, bass.ds(e, 1)],
                                             xs_sb[:, s, j, CW:CW + K], ALU.is_equal, ALU.mult, accum_out=wtok[:, s, j:j + 1])
                dve.tensor_copy(toki[:, s, :], xs_sb[:, s, :, CT]).then_inc(tok_ready, 1)

            def expert_hidden(e, par, first):
                if not first:
                    dve.wait_ge(y_done, e - 1)
                dve.wait_ge(silA_done, e + 1)
                dve.tensor_tensor(hid0[:, par], sil0[:, par], pA[par][:, CAP:2 * CAP], ALU.mult)
                dve.wait_ge(silC_done, e + 1)
                dve.tensor_tensor(hid1[:, par], sil1[:, par], pC[par][64:64 + F1, 0:CAP], ALU.mult).then_inc(xhid_ready, 1)

            def weigh(e, s):
                par = s % 2
                dve.wait_ge(tok_ready, e + 1)
                dve.wait_ge(y_done, e + 1)
                for j in range(2):
                    m = dve.tensor_scalar(y_sb[:, s, j, :], pY[par][:, j * D:(j + 1) * D], wtok[:, s, j:j + 1], None, ALU.mult)
                m.then_inc(y_ready, 1)

            weights(0, 0, True)
            weights(0, 1, True)
            expert_hidden(0, 0, True)
            weights(0, 2, True)
            expert_hidden(1, 1, True)
            weigh(0, 0)
            weights(0, 3, True)
            expert_hidden(2, 0, False)
            weigh(1, 1)
            with dve.Fori(1, E // 4) as i:
                for s in range(4):
                    weights(i, s, False)
                    expert_hidden(4 * i + s - 1, (s - 1) % 2, False)
                    weigh(4 * i + s - 2, (s - 2) % 4)
            expert_hidden(E - 1, 1, False)
            weigh(E - 2, 2)
            weigh(E - 1, 3)

            dve.wait_ge(added[0][0], 16 * (E // 2))
            with dve.Fori(0, n) as b:
                dve.tensor_copy(ovcol[:, 0:1], rows_f[:, 2, bass.ds(b, 1)]).then_inc(o_col, 1)
                dve.wait_ge(o_x, 16 * b + 16)
                dve.wait_ge(o_col, b + 1)
                alone(dve, "dve")
                dve.scalar_tensor_tensor(wsel[:, 0, 0, :], xs_sb[:, 0, 0, CE:CE + K], ovcol[:, 0:1],
                                         xs_sb[:, 0, 0, CW:CW + K], ALU.is_equal, ALU.mult, accum_out=wtok[:, 0, 0:1])
                dve.tensor_copy(toki[:, 0, 0:1], xs_sb[:, 0, 0, CT:CT + 1]).then_inc(o_tok, 1)
                dve.wait_ge(o_silu, b + 1)
                dve.tensor_tensor(hid0[:, 0, 0:P], sil0[:, 0, 0:P], pA[0][:, P:2 * P], ALU.mult)
                dve.tensor_tensor(hid1[:, 0, 0:P], sil1[:, 0, 0:P], pC[0][64:64 + F1, 0:P], ALU.mult).then_inc(o_hid, 1)
                dve.wait_ge(o_tok, b + 1)
                dve.wait_ge(o_y, b + 1)
                dve.tensor_scalar(y_sb[:, 0, 0, :], pY[0][:, 0:D], wtok[:, 0, 0:1], None, ALU.mult).then_inc(o_yr, 1)
                dve.wait_ge(o_add, 16 * b + 16)
                alone(dve, "dve")

            dve.wait_ge(early_in, 48)
            for c in range(3):
                xc = X[:, 4 * c:4 * c + 4, :]
                for q in (1, 2, 3, 0):
                    if q == 0:
                        dve.wait_ge(back_in[c], 16)
                    m = dve.tensor_tensor(xc, xc, back[q][:, 4 * c:4 * c + 4, :], ALU.add)
                    if q:
                        link(m)
                m.then_inc(sum_done, 1)


def kernel(**inputs):
    import numpy as np
    import concourse.bacc as bacc
    from concourse.bass_utils import run_bass_kernel_spmd

    def toeplitz(k):
        p = np.concatenate([np.zeros((16, 128), k.dtype), k], 1)
        i = np.arange(128)[None, None, :] - np.arange(128)[None, :, None]
        return np.stack([p[:, 128 + i[0]], p[:, 256 + i[0]]], 2).reshape(16, 128, 256)

    def expert_weights(w, down):
        w = w.reshape(64, 352, 2, 128).transpose(0, 3, 2, 1)
        o = np.zeros((64, 128, 2, 368), w.dtype)
        o[..., 0:128] = w[..., 0:128]
        o[..., 128:256] = w[..., 176:304]
        o[..., 256:304] = w[..., 128:176]
        o[..., 320:368] = w[..., 304:352]
        return np.concatenate([o.reshape(64, 128, 736), down[:, 0:128]], 2)

    a = {k: np.asarray(v) for k, v in inputs.items()}
    c = a["ctx_2048"]
    down = a["L1_ffn_w_down"].transpose(0, 2, 1)
    arrays = {
        "x": a["x"],
        "ctxn": c,
        "ctxT": c.transpose(0, 2, 1),
        "ctxH": c.reshape(16, 16, 8, 2, 128).transpose(1, 4, 3, 0, 2).reshape(16, 128, 256),
        "toep": toeplitz(a["L1_xattn_ssm_kernel"]),
        "gates": np.stack([a["g_xattn"], a["g_ffn"]], 1).reshape(4),
        "wsynT": a["L0_ffn_W_syn"].T,
        "woutT": a["L0_ffn_W_out"].T,
        "bsyn": a["L0_ffn_b_syn"],
        "bout": a["L0_ffn_b_out"],
        "gamma": a["L0_ffn_gamma"],
        "beta": a["L0_ffn_beta"],
        "ssm_D": a["L1_xattn_D"],
        "gateT": a["L1_ffn_gate_w"].reshape(64, 2, 128).transpose(2, 1, 0),
        "wexp": expert_weights(a["L1_ffn_w_gate_up"], down),
        "wd1": down[:, 128:],
        "wsgu": a["L1_ffn_ws_gate_up"].reshape(704, 2, 128).transpose(2, 1, 0),
        "wsd": a["L1_ffn_ws_down"].T,
    }
    arrays = {"in_" + k: np.ascontiguousarray(v) for k, v in arrays.items()}
    nc = bacc.Bacc("TRN2", target_bir_lowering=False, num_devices=1)
    args = [nc.dram_tensor(n, v.shape, mybir.dt.from_np(v.dtype), kind="ExternalInput").ap() for n, v in arrays.items()]
    args.append(nc.dram_tensor("out_0", (16, 128, 256), mybir.dt.float32, kind="ExternalOutput").ap())
    build(nc, *args)
    r = run_bass_kernel_spmd(nc, [arrays], core_ids=[0])
    return r.results[0]["out_0"]
```
